# Optimizing a Trainium2 kernel written in Bass

```python
import numpy as np
import jax
import jax.numpy as jnp

def _softmax(x, axis=-1):
    return jax.nn.softmax(x, axis=axis)

def _gelu(x):
    return jax.nn.gelu(x, approximate=True)

def _silu(x):
    return jax.nn.silu(x)

def _sigmoid(x):
    return jax.nn.sigmoid(x)

def _layernorm(x, axis=-1, eps=1e-05):
    m = jnp.mean(x, axis=axis, keepdims=True)
    v = jnp.var(x, axis=axis, keepdims=True)
    return (x - m) / jnp.sqrt(v + eps)

def _scatter_add(tgt, idx, src, axis=0):
    return tgt.at[idx].add(src)

def _segment_sum(src, seg, n):
    return jax.ops.segment_sum(src, seg, n)
kernel_name = 'mk_adj_preln_d2_adj_r2_637f2f'

def setup_inputs(seed: int=0):
    np.random.seed(seed)
    _w = jnp.asarray

    def _rec_inputs():
        import jax
        import jax.numpy as jnp
        _gk = jax.random.key(seed)
        x = -0.0002928 + 1 * jax.random.normal(jax.random.fold_in(_gk, 1), (32, 256, 128), jnp.float32)
        _a = jax.random.bernoulli(jax.random.fold_in(_gk, 2), 0.03125, (32, 256, 256))
        _a = jnp.logical_or(_a, jnp.swapaxes(_a, -1, -2))
        _a = jnp.logical_or(_a, jnp.eye(256, dtype=bool))
        _af = _a.astype(jnp.float32)
        _af = _af * jax.random.uniform(jax.random.fold_in(_gk, 3), (32, 256, 256), jnp.float32, 0.05, 1)
        adj = _af
        return (x, adj)
    x, adj = _rec_inputs()

    def _L0_gnn_setup():
        import jax, jax.numpy as jnp
        import numpy as np
        key = jax.random.key(seed)
        k1, k2, k3, k4 = jax.random.split(key, 4)
        B, N, F_in, F_out = (8, 1024, 128, 128)
        inp = jax.random.normal(k1, (B, N, F_in), dtype=jnp.float32)
        adj = jax.random.uniform(k2, (B, N, N), dtype=jnp.float32)
        stdv = 1.0 / np.sqrt(F_out)
        weight = jax.random.uniform(k3, (F_in, F_out), dtype=jnp.float32, minval=-stdv, maxval=stdv)
        bias = jax.random.uniform(k4, (F_out,), dtype=jnp.float32, minval=-stdv, maxval=stdv)
        return {'input': inp, 'adj': adj, 'weight': weight, 'bias': bias}
    _L0_gnn_all = _L0_gnn_setup()
    _L0_gnn_in = {k: v for k, v in _L0_gnn_all.items() if k in ('weight', 'bias')}
    del _L0_gnn_all

    def _L1_gnn_setup():
        import jax, jax.numpy as jnp
        import numpy as np
        from jax import lax
        DIM = 128
        EPS = 1e-05

        def _bn(h, g, b, m, v):
            scale = g / jnp.sqrt(v + EPS)
            return h * scale[None, :, None] + (b - m * scale)[None, :, None]

        def _conv1d(h, w, pad):
            return lax.conv_general_dilated(h, w, window_strides=(1,), padding=[(pad, pad)], dimension_numbers=('NCH', 'OIH', 'NCH'))
        key = jax.random.key(seed)
        ks = jax.random.split(key, 16)
        bs, n, d = (16, 1024, DIM)
        s = 0.05
        return {'x': jax.random.normal(ks[0], (bs, n, d), jnp.float32), 'mask': jnp.ones((bs, n, n), jnp.float32), 'w_se': jax.random.normal(ks[1], (3, d), jnp.float32) * s, 'b_se': jnp.zeros((3,), jnp.float32), 'conv1_w': jax.random.normal(ks[2], (d, d, 1), jnp.float32) * s, 'bn1_g': jnp.ones((d,), jnp.float32), 'bn1_b': jnp.zeros((d,), jnp.float32), 'bn1_m': jnp.zeros((d,), jnp.float32), 'bn1_v': jnp.ones((d,), jnp.float32), 'conv2_w': jax.random.normal(ks[3], (d, d, 17), jnp.float32) * s, 'bn2_g': jnp.ones((d,), jnp.float32), 'bn2_b': jnp.zeros((d,), jnp.float32), 'bn2_m': jnp.zeros((d,), jnp.float32), 'bn2_v': jnp.ones((d,), jnp.float32), 'w_msg': jax.random.normal(ks[4], (d, d), jnp.float32) * s, 'b_msg': jnp.zeros((d,), jnp.float32), 'w_ih': jax.random.normal(ks[5], (3 * d, 2 * d), jnp.float32) * s, 'b_ih': jnp.zeros((3 * d,), jnp.float32), 'w_hh': jax.random.normal(ks[6], (3 * d, d), jnp.float32) * s, 'b_hh': jnp.zeros((3 * d,), jnp.float32)}
    _L1_gnn_all = _L1_gnn_setup()
    _L1_gnn_in = {k: v for k, v in _L1_gnn_all.items() if k in ('w_se', 'b_se', 'conv1_w', 'bn1_g', 'bn1_b', 'bn1_m', 'bn1_v', 'conv2_w', 'bn2_g', 'bn2_b', 'bn2_m', 'bn2_v', 'w_msg', 'b_msg', 'w_ih', 'b_ih', 'w_hh', 'b_hh')}
    del _L1_gnn_all
    return {'x': x, 'adj': adj, 'L0_gnn_weight': _L0_gnn_in['weight'], 'L0_gnn_bias': _L0_gnn_in['bias'], 'L1_gnn_w_se': _L1_gnn_in['w_se'], 'L1_gnn_b_se': _L1_gnn_in['b_se'], 'L1_gnn_conv1_w': _L1_gnn_in['conv1_w'], 'L1_gnn_bn1_g': _L1_gnn_in['bn1_g'], 'L1_gnn_bn1_b': _L1_gnn_in['bn1_b'], 'L1_gnn_bn1_m': _L1_gnn_in['bn1_m'], 'L1_gnn_bn1_v': _L1_gnn_in['bn1_v'], 'L1_gnn_conv2_w': _L1_gnn_in['conv2_w'], 'L1_gnn_bn2_g': _L1_gnn_in['bn2_g'], 'L1_gnn_bn2_b': _L1_gnn_in['bn2_b'], 'L1_gnn_bn2_m': _L1_gnn_in['bn2_m'], 'L1_gnn_bn2_v': _L1_gnn_in['bn2_v'], 'L1_gnn_w_msg': _L1_gnn_in['w_msg'], 'L1_gnn_b_msg': _L1_gnn_in['b_msg'], 'L1_gnn_w_ih': _L1_gnn_in['w_ih'], 'L1_gnn_b_ih': _L1_gnn_in['b_ih'], 'L1_gnn_w_hh': _L1_gnn_in['w_hh'], 'L1_gnn_b_hh': _L1_gnn_in['b_hh']}

def reference(x, adj, L0_gnn_weight, L0_gnn_bias, L1_gnn_w_se, L1_gnn_b_se, L1_gnn_conv1_w, L1_gnn_bn1_g, L1_gnn_bn1_b, L1_gnn_bn1_m, L1_gnn_bn1_v, L1_gnn_conv2_w, L1_gnn_bn2_g, L1_gnn_bn2_b, L1_gnn_bn2_m, L1_gnn_bn2_v, L1_gnn_w_msg, L1_gnn_b_msg, L1_gnn_w_ih, L1_gnn_b_ih, L1_gnn_w_hh, L1_gnn_b_hh):
    import jax
    import jax.numpy as jnp

    def _L0_gnn_ref(input, adj, weight, bias):
        import jax, jax.numpy as jnp
        import numpy as np
        d = adj.sum(axis=1) ** (-0.5)
        adj_norm = d[:, :, None] * adj * d[:, None, :]
        support = jnp.einsum('bnf,fo->bno', input, weight)
        output = jnp.einsum('bnm,bmo->bno', adj_norm, support) + bias
        return output

    def _L1_gnn_ref(x, mask, w_se, b_se, conv1_w, bn1_g, bn1_b, bn1_m, bn1_v, conv2_w, bn2_g, bn2_b, bn2_m, bn2_v, w_msg, b_msg, w_ih, b_ih, w_hh, b_hh):
        import jax, jax.numpy as jnp
        import numpy as np
        from jax import lax
        DIM = 128
        EPS = 1e-05

        def _bn(h, g, b, m, v):
            scale = g / jnp.sqrt(v + EPS)
            return h * scale[None, :, None] + (b - m * scale)[None, :, None]

        def _conv1d(h, w, pad):
            return lax.conv_general_dilated(h, w, window_strides=(1,), padding=[(pad, pad)], dimension_numbers=('NCH', 'OIH', 'NCH'))
        d = x.shape[-1]
        xc = jnp.transpose(x, (0, 2, 1))
        h = _bn(_conv1d(xc, conv1_w, 0), bn1_g, bn1_b, bn1_m, bn1_v)
        h = jax.nn.relu(h)
        h = _bn(_conv1d(h, conv2_w, 8), bn2_g, bn2_b, bn2_m, bn2_v)
        x_conv = jnp.transpose(jax.nn.relu(h + xc), (0, 2, 1))
        s = x @ w_se.T + b_se
        sq = jnp.sum(s * s, axis=-1)
        dist = sq[:, :, None] + sq[:, None, :] - 2.0 * jnp.einsum('bnd,bmd->bnm', s, s)
        A = jnp.exp(-dist) * mask
        msg = jax.nn.relu(x @ w_msg.T + b_msg)
        x_nmp = jnp.einsum('bnm,bmd->bnd', A, msg)
        x_in = jnp.concatenate([x_conv, x_nmp], axis=-1)
        gi = x_in @ w_ih.T + b_ih
        gh = x @ w_hh.T + b_hh
        gi_r, gi_z, gi_n = (gi[..., :d], gi[..., d:2 * d], gi[..., 2 * d:])
        gh_r, gh_z, gh_n = (gh[..., :d], gh[..., d:2 * d], gh[..., 2 * d:])
        r = jax.nn.sigmoid(gi_r + gh_r)
        z = jax.nn.sigmoid(gi_z + gh_z)
        nn_ = jnp.tanh(gi_n + r * gh_n)
        return (1.0 - z) * nn_ + z * x
    h = jnp.maximum(_layernorm(x, axis=-1), 0.0)
    x = x + _L0_gnn_ref(h, adj, L0_gnn_weight, L0_gnn_bias)
    h = jnp.maximum(_layernorm(x, axis=-1), 0.0)
    x = x + _L1_gnn_ref(h, adj, L1_gnn_w_se, L1_gnn_b_se, L1_gnn_conv1_w, L1_gnn_bn1_g, L1_gnn_bn1_b, L1_gnn_bn1_m, L1_gnn_bn1_v, L1_gnn_conv2_w, L1_gnn_bn2_g, L1_gnn_bn2_b, L1_gnn_bn2_m, L1_gnn_bn2_v, L1_gnn_w_msg, L1_gnn_b_msg, L1_gnn_w_ih, L1_gnn_b_ih, L1_gnn_w_hh, L1_gnn_b_hh)
    return x

_drawn_inputs = setup_inputs


def setup_inputs(seed=0):
    import zlib

    import numpy as np

    out = dict(_drawn_inputs(seed))
    spreads = {'L1_gnn_b_se': (0.0, 2.0),
     'L1_gnn_bn1_g': (1.0, 0.6),
     'L1_gnn_bn1_b': (0.0, 0.347),
     'L1_gnn_bn1_m': (0.0, 0.327),
     'L1_gnn_bn1_v': (1.0, 0.6),
     'L1_gnn_bn2_g': (1.0, 0.6),
     'L1_gnn_bn2_b': (0.0, 0.624),
     'L1_gnn_bn2_m': (0.0, 0.522),
     'L1_gnn_bn2_v': (1.0, 0.6),
     'L1_gnn_b_msg': (0.0, 0.1),
     'L1_gnn_b_ih': (0.0, 0.283),
     'L1_gnn_b_hh': (0.0, 0.409)}
    factors = {}
    for name, (base, spread) in spreads.items():
        noise = np.random.default_rng([zlib.crc32(name.encode()), seed]).standard_normal(out[name].shape)
        drawn = base * np.exp(spread * noise) if base else spread * noise
        out[name] = jnp.asarray(drawn.astype(out[name].dtype))
    for name, factor in factors.items():
        out[name] = (out[name] * factor).astype(out[name].dtype)
    return out
```

```python
from contextlib import ExitStack

import concourse.bass as bass
from concourse import mybir

P = 128
TAPS = 17
PAD = TAPS // 2
LN_EPS = 1e-5
BN_EPS = 1e-5

F32 = mybir.dt.float32
F32R = mybir.dt.float32r
ACT = mybir.ActivationFunctionType
ALU = mybir.AluOpType

BN1_G, BN1_B, BN1_M, BN1_V, BN2_G, BN2_B, BN2_M, BN2_V, IH_R, IH_Z, IH_N, HH_R, HH_Z, HH_N = range(14)
ROW_BIAS0, ROW_BMSG = range(2)


def build_program(nc, x, adj, w0_in, w1_in, w2_in, wse_in, bse_in, wmsg_in, wih_in, whh_in, cols_in, rows_in, y):
    B, N, D = x.shape
    assert D == P and N == 2 * P and B % 2 == 0
    PAIRS = B // 2
    TILES = 2 * N // P
    NT = N // P
    COLS = 2 * N
    KQ = 3 * 32

    W0 = 0
    W1 = W0 + P
    WS = W1 + P
    WM = WS + KQ
    WHH = WM + P
    WIH = WHH + 3 * P
    W2 = WIH + 6 * P
    WEND = W2 + TAPS * P

    with ExitStack() as ctx:
        def sb(name, shape, dt=F32):
            return ctx.enter_context(nc.sbuf_tensor(name, shape, dt))

        def sem(name):
            return ctx.enter_context(nc.semaphore(name))

        bank = [ctx.enter_context(nc.psum_tensor(f"bank{b}", [P, COLS], F32)) for b in range(8)]
        ps_c1, ps_s, ps_msg, ps_u, ps_conv, ps_out = bank[4], bank[5], bank[6], bank[1], bank[0], bank[7]
        ps_kernel, ps_yT, ps_hT, ps_adjT = bank[2:4], bank[7], bank[1], bank[2:4]
        ps_nmp, ps_ghn, ps_r, ps_z, ps_gin = bank[5], bank[7], bank[4], bank[6], bank[0]

        w_f = sb("w_f", [P, WEND])
        w_hi = sb("w_hi", [P, WEND], F32R)
        w_lo = sb("w_lo", [P, WEND], F32R)
        cols = sb("cols", [P, 14])
        rows = sb("rows", [P, 2, P])
        bse = sb("bse", [KQ, 1])
        bn_scale_row = sb("bn_scale_row", [P, 2, P])
        bn_scale_col = sb("bn_scale_col", [P, 2])
        bn_shift = sb("bn_shift", [P, 2])
        gate_bias = sb("gate_bias", [P, 3])
        minus_half = sb("minus_half", [P, 2, TILES])
        ones = sb("ones", [P, P])
        bn_diag = sb("bn_diag", [P, 2, P])
        ident = sb("ident", [P, P])

        X = [sb(f"X{q}", [P, TILES, P]) for q in range(2)]
        ADJ = [sb(f"ADJ{q}", [P, 2, NT, N]) for q in range(2)]
        adjT = [sb(f"adjT{q}", [P, 2, NT, N]) for q in range(2)]
        stats0 = sb("stats0", [P, TILES, 6])
        parts0 = sb("parts0", [P, TILES, 5])
        mean0 = sb("mean0", [P, TILES])
        powers0 = sb("powers0", [P, 2, TILES])
        roots0 = sb("roots0", [P, 2, TILES])
        scale0 = sb("scale0", [P, TILES])
        deg = [sb(f"deg{q}", [P, TILES]) for q in range(2)]
        xn0 = sb("xn0", [P, TILES, P])
        h0 = sb("h0", [P, TILES, P])
        uT_hi = sb("uT_hi", [P, COLS], F32R)
        uT_lo = sb("uT_lo", [P, COLS], F32R)
        xb = sb("xb", [P, TILES, P])
        X1 = [sb(f"X1_{q}", [P, TILES, P]) for q in range(2)]

        stats1 = sb("stats1", [P, TILES, 6])
        parts1 = sb("parts1", [P, TILES, 5])
        mean1 = sb("mean1", [P, TILES])
        power1 = sb("power1", [P, TILES])
        rstd1 = sb("rstd1", [P, TILES])
        xn1 = sb("xn1", [P, TILES, P])
        hT = [sb(f"hT{q}", [P, COLS]) for q in range(2)]
        hT_hi = [sb(f"hT_hi{q}", [P, COLS], F32R) for q in range(2)]
        hT_lo = [sb(f"hT_lo{q}", [P, COLS], F32R) for q in range(2)]
        c1 = sb("c1", [P, COLS])
        c1_hi = sb("c1_hi", [P, 2, N + 2 * PAD], F32R)
        c1_lo = sb("c1_lo", [P, 2, N + 2 * PAD], F32R)
        kL = sb("kL", [KQ, COLS])
        kR = sb("kR", [KQ, COLS])
        msg_b = sb("msg_b", [P, TILES, P])
        msg = sb("msg", [P, TILES, P])
        kern = sb("kern", [P, 2, NT, N])
        edges = sb("edges", [P, 2, NT, N])
        cr = sb("cr", [P, COLS])
        xc_hi = sb("xc_hi", [P, COLS], F32R)
        xc_lo = sb("xc_lo", [P, COLS], F32R)
        nmp_hi = sb("nmp_hi", [P, COLS], F32R)
        nmp_lo = sb("nmp_lo", [P, COLS], F32R)
        half_ghn = sb("half_ghn", [P, COLS])
        tanh_r = sb("tanh_r", [P, COLS])
        tanh_z = sb("tanh_z", [P, COLS])
        rg = sb("rg", [P, COLS])
        n_in = sb("n_in", [P, COLS])
        n_gate = sb("n_gate", [P, COLS])
        h_minus_n = sb("h_minus_n", [P, COLS])
        z_part = sb("z_part", [P, COLS])
        yT = sb("yT", [P, COLS])
        OUT = [sb(f"OUT{q}", [P, TILES, P]) for q in range(2)]

        weights_in = [sem(f"weights_in{c}") for c in range(3)]
        wse_zero, wse_in_place = sem("wse_zero"), sem("wse_in_place")
        pool_prep, dve_prep = sem("pool_prep"), sem("dve_prep")
        ident_ready, consts_ready = sem("ident_ready"), sem("consts_ready")
        weights_hi, weights_lo = sem("weights_hi"), sem("weights_lo")
        scaled, scaled_cols, diag_ready, bn_rows_done, vectors_ready = sem("scaled"), sem("scaled_cols"), sem("diag_ready"), sem("bn_rows_done"), sem("vectors_ready")
        x_loaded = [sem(f"x_loaded{q}") for q in range(2)]
        adj_loaded = [sem(f"adj_loaded{q}") for q in range(2)]
        y_stored = [sem(f"y_stored{q}") for q in range(2)]
        adjT_done, u_done, out_done, hT_done = sem("adjT_done"), sem("u_done"), sem("out_done"), sem("hT_done")
        c1_done, s_done, msg_done, conv_done = sem("c1_done"), sem("s_done"), sem("msg_done"), sem("conv_done")
        kernel_done, nmp_done, ghn_done = sem("kernel_done"), sem("nmp_done"), sem("ghn_done")
        r_done, z_done, gin_done, yT_done = sem("r_done"), sem("z_done"), sem("gin_done"), sem("yT_done")
        adjT_copied, h0_ready, uT_hi_ready, hT_ready = sem("adjT_copied"), sem("h0_ready"), sem("uT_hi_ready"), sem("hT_ready")
        c1_ready, k_by_act, kern_ready, xc_hi_ready = sem("c1_ready"), sem("k_by_act"), sem("kern_ready"), sem("xc_hi_ready")
        nmp_hi_ready, half_ghn_ready = sem("nmp_hi_ready"), sem("half_ghn_ready")
        tanh_r_ready, tanh_z_ready, n_ready = sem("tanh_r_ready"), sem("tanh_z_ready"), sem("n_ready")
        stats0_ready, xn0_ready = sem("stats0_ready"), sem("xn0_ready")
        uT_lo_ready, x1_ready = sem("uT_lo_ready"), sem("x1_ready")
        stats1_ready, xn1_ready = sem("stats1_ready"), sem("xn1_ready")
        hT_hi_ready, c1_hi_ready, k_by_dve, msg_b_ready = sem("hT_hi_ready"), sem("c1_hi_ready"), sem("k_by_dve"), sem("msg_b_ready")
        edges_ready = sem("edges_ready")
        cr_ready, xc_lo_ready, nmp_lo_ready = sem("cr_ready"), sem("xc_lo_ready"), sem("nmp_lo_ready")
        rg_ready, n_in_ready, z_part_ready, yT_ready, out_ready = sem("rg_ready"), sem("n_in_ready"), sem("z_part_ready"), sem("yT_ready"), sem("out_ready")
        deg_ready, roots0_ready, scale0_ready, xb_ready = sem("deg_ready"), sem("roots0_ready"), sem("scale0_ready"), sem("xb_ready")
        rstd1_ready, hT_lo_ready, c1_lo_ready = sem("rstd1_ready"), sem("hT_lo_ready"), sem("c1_lo_ready")
        msg_ready, hn_ready = sem("msg_ready"), sem("hn_ready")

        def loads_of(n, q):
            return 8 * (n - q) + 16

        x_pairs = x.rearrange("(n b) (t p) d -> n p (b t) d", b=2, p=P)
        y_pairs = y.rearrange("(n b) (t p) d -> n p (b t) d", b=2, p=P)
        adj_pairs = adj.rearrange("(n b) (t p) m -> n p b t m", b=2, p=P)

        def sweep(eng, step):
            step(0, 0)
            steady = (PAIRS - 3) // 2 * 2
            with eng.Fori(1, 1 + steady, 2) as i:
                step(i, 1)
                step(i + 1, 0)
            for n in range(1 + steady, PAIRS):
                step(n, n % 2)

        def exists(n):
            return not isinstance(n, int) or 0 <= n < PAIRS

        block = ctx.enter_context(nc.Block())

        @block.sync
        def _(sp):
            def load(n, q):
                sp.dma_start(ADJ[q][:, 0], adj_pairs[n, :, 0]).then_inc(adj_loaded[q], 16)
                sp.dma_start(ADJ[q][:, 1], adj_pairs[n, :, 1]).then_inc(adj_loaded[q], 16)
                sp.dma_start(X[q][:], x_pairs[n]).then_inc(x_loaded[q], 16)

            for q in range(2):
                sp.sem_inc(y_stored[q], 16)
            load(0, 0)
            sp.dma_start(rows[:], rows_in.unsqueeze(0).broadcast_to([P, 2, P])).then_inc(weights_in[0], 16)
            sp.dma_start(w_f[:, W0:W0 + P], w0_in).then_inc(weights_in[0], 16)
            sp.dma_start(cols[:], cols_in).then_inc(weights_in[0], 16)
            load(1, 1)
            sp.dma_start(w_f[:, W2:WEND], w2_in).then_inc(weights_in[2], 16)

            def step(i, q):
                if exists(i + 2):
                    sp.wait_ge(adjT_done, 2 * (i + 1))
                    sp.wait_ge(xn0_ready, i + 1)
                    sp.wait_ge(xb_ready, i + 1)
                    load(i + 2, q)
                if exists(i - 1):
                    sp.wait_ge(out_ready, i)
                    sp.dma_start(y_pairs[i - 1], OUT[1 - q][:]).then_inc(y_stored[1 - q], 16)

            sweep(sp, step)
            sp.wait_ge(out_ready, PAIRS)
            sp.dma_start(y_pairs[PAIRS - 1], OUT[(PAIRS - 1) % 2][:]).then_inc(y_stored[(PAIRS - 1) % 2], 16)
            for q in range(2):
                sp.wait_ge(y_stored[q], 16 * (PAIRS // 2 + 1))

        @block.tensor
        def _(pe):
            def w(part, at, width=P):
                return part[:, at:at + width]

            def product(out, left, right, first, last):
                (lh, ll), (rh, rl) = left, right
                pe.matmul(out, lh, rh, start=first, stop=False)
                pe.matmul(out, ll, rh, start=False, stop=False)
                return pe.matmul(out, lh, rl, start=False, stop=last)

            def weight(at, width=P):
                return w(w_hi, at, width), w(w_lo, at, width)

            def transpose_adj(n, q):
                pe.wait_ge(adj_loaded[q], 2 * loads_of(n, q))
                for b in range(2):
                    pe_bank = ps_adjT[b][:].rearrange("p (m n) -> p m n", m=NT)
                    for mt in range(NT):
                        for nt in range(NT):
                            last = pe.transpose(pe_bank[:, mt, nt * P:(nt + 1) * P],
                                                ADJ[q][:, b, nt, mt * P:(mt + 1) * P], ident[:])
                    last.then_inc(adjT_done, 1)

            def aggregate(n, q):
                pe.wait_ge(h0_ready, n + 1)
                pe.wait_ge(adjT_copied, 4 * (n + 1))
                for b in range(2):
                    for mt in range(NT):
                        last = pe.matmul(ps_u[:, b * N:(b + 1) * N], h0[:, b * NT + mt, :], adjT[q][:, b, mt, :],
                                         start=(mt == 0), stop=(mt == NT - 1))
                last.then_inc(u_done, 1)

            def project(n):
                pe.wait_ge(uT_lo_ready, n + 1)
                for t in range(TILES):
                    c = slice(t * P, (t + 1) * P)
                    last = product(ps_out[:, c], (uT_hi[:, c], uT_lo[:, c]), weight(W0), True, True)
                last.then_inc(out_done, 1)

            def transpose_h(n):
                pe.wait_ge(xn1_ready, n + 1)
                for t in range(TILES):
                    last = pe.transpose(ps_hT[:, t * P:(t + 1) * P], xn1[:, t, :], ident[:])
                last.then_inc(hT_done, 1)

            def transpose_y(n):
                pe.wait_ge(yT_ready, n + 1)
                for t in range(TILES):
                    last = pe.transpose(ps_yT[:, t * P:(t + 1) * P], yT[:, t * P:(t + 1) * P], ident[:])
                last.then_inc(yT_done, 1)

            def head(n, q):
                hp = (hT_hi[q][:], hT_lo[q][:])
                pe.wait_ge(hT_hi_ready, n + 1)
                pe.wait_ge(hT_lo_ready, n + 1)
                if exists(n - 1):
                    pe.wait_ge(tanh_r_ready, n)
                product(ps_c1[:], weight(W1), hp, True, True).then_inc(c1_done, 1)
                product(ps_s[0:KQ, :], weight(WS, KQ), hp, True, True).then_inc(s_done, 1)
                if exists(n - 1):
                    pe.wait_ge(tanh_z_ready, n)
                for t in range(TILES):
                    c = slice(t * P, (t + 1) * P)
                    last = product(ps_msg[:, c], (hT_hi[q][:, c], hT_lo[q][:, c]), weight(WM), True, True)
                last.then_inc(msg_done, 1)

            def conv(n, a, b):
                for k in range(a, b):
                    part, tap = divmod(k, TAPS)
                    if k == 0:
                        pe.wait_ge(c1_hi_ready, n + 1)
                        if exists(n - 1):
                            pe.wait_ge(n_in_ready, n)
                    if k == 2 * TAPS:
                        pe.wait_ge(c1_lo_ready, n + 1)
                    left = w(w_lo if part == 1 else w_hi, W2 + tap * P)
                    right = (c1_lo if part == 2 else c1_hi)[:, :, tap:tap + N]
                    last = pe.matmul(ps_conv[:].rearrange("p (b n) -> p b n", b=2), left, right,
                                     start=(k == 0), stop=(k == 3 * TAPS - 1))
                if b == 3 * TAPS:
                    last.then_inc(conv_done, 1)

            def distances(n):
                pe.wait_ge(k_by_act, 3 * (n + 1))
                pe.wait_ge(k_by_dve, n + 1)
                for b in range(2):
                    for mt in range(NT):
                        c = b * N + mt * P
                        last = pe.matmul(ps_kernel[b][:, mt * N:(mt + 1) * N], kL[:, c:c + P], kR[:, b * N:(b + 1) * N],
                                         start=True, stop=True)
                    last.then_inc(kernel_done, 1)

            def messages(n):
                pe.wait_ge(edges_ready, 2 * (n + 1))
                pe.wait_ge(msg_ready, n + 1)
                for b in range(2):
                    for mt in range(NT):
                        last = pe.matmul(ps_nmp[:, b * N:(b + 1) * N], msg[:, b * NT + mt, :], edges[:, b, mt, :],
                                         start=(mt == 0), stop=(mt == NT - 1))
                last.then_inc(nmp_done, 1)

            def gates(n, q):
                hp, cp, mp = (hT_hi[q][:], hT_lo[q][:]), (xc_hi[:], xc_lo[:]), (nmp_hi[:], nmp_lo[:])
                r, z, g = 0, P, 2 * P
                product(ps_ghn[:], weight(WHH + g), hp, True, True).then_inc(ghn_done, 1)
                product(ps_r[:], weight(WHH + r), hp, True, False)
                product(ps_z[:], weight(WHH + z), hp, True, False)
                pe.wait_ge(xc_hi_ready, n + 1)
                pe.wait_ge(xc_lo_ready, n + 1)
                product(ps_r[:], weight(WIH + r), cp, False, False)
                pe.wait_ge(nmp_hi_ready, n + 1)
                pe.wait_ge(nmp_lo_ready, n + 1)
                product(ps_r[:], weight(WIH + 3 * P + r), mp, False, True).then_inc(r_done, 1)
                product(ps_z[:], weight(WIH + z), cp, False, False)
                product(ps_z[:], weight(WIH + 3 * P + z), mp, False, True).then_inc(z_done, 1)
                product(ps_gin[:], weight(WIH + g), cp, True, False)
                product(ps_gin[:], weight(WIH + 3 * P + g), mp, False, True).then_inc(gin_done, 1)

            pe.wait_ge(ident_ready, 1)
            transpose_adj(0, 0)
            aggregate(0, 0)
            pe.wait_ge(weights_lo, 1)
            project(0)
            transpose_h(0)
            transpose_adj(1, 1)
            pe.wait_ge(diag_ready, 2)
            pe.matmul(ps_conv[:, 0:2 * P], ones[:], bn_diag[:].rearrange("p v o -> p (v o)"),
                      start=True, stop=True).then_inc(bn_rows_done, 1)
            pe.wait_ge(weights_lo, 3)
            pe.wait_ge(consts_ready, 7)

            def step(i, q):
                head(i, q)
                if exists(i + 1):
                    pe.wait_ge(hT_ready, i + 1)
                    aggregate(i + 1, 1 - q)
                conv(i, 0, 8)
                if exists(i - 1):
                    pe.wait_ge(half_ghn_ready, i)
                    transpose_y(i - 1)
                conv(i, 8, 13)
                if exists(i + 1):
                    if exists(i - 1):
                        pe.wait_ge(out_ready, i)
                    project(i + 1)
                conv(i, 13, 18)
                distances(i)
                conv(i, 18, 3 * TAPS)
                if exists(i + 1):
                    transpose_h(i + 1)
                pe.wait_ge(kern_ready, 2 * (i + 1))
                if exists(i + 2):
                    transpose_adj(i + 2, q)
                messages(i)
                if exists(i + 1):
                    pe.wait_ge(x1_ready, i + 2)
                else:
                    pe.wait_ge(out_ready, i)
                gates(i, q)

            sweep(pe, step)
            transpose_y(PAIRS - 1)

        @block.scalar
        def _(act):
            act.dma_start(w_f[:, W1:W1 + P], w1_in).then_inc(weights_in[1], 16)
            act.dma_start(w_f[:, WM:WM + P], wmsg_in).then_inc(weights_in[1], 16)
            act.dma_start(w_f[:, WHH:WIH], whh_in).then_inc(weights_in[1], 16)
            act.dma_start(w_f[:, WIH:W2].rearrange("p (c g) -> p c g", c=2), wih_in).then_inc(weights_in[1], 16)
            act.wait_ge(wse_zero, 2)
            for g in range(3):
                act.dma_start(w_f[:, WS + 32 * g:WS + 32 * g + 3], wse_in).then_inc(wse_in_place, 16)
                act.dma_start(bse[32 * g:32 * g + 3, :], bse_in).then_inc(wse_in_place, 16)

            def copy_adj(n, q):
                for b in range(2):
                    act.wait_ge(adjT_done, 2 * n + b + 1)
                    if b == 0:
                        act.wait_ge(roots0_ready, n)
                    for mt in range(NT):
                        t = b * NT + mt
                        act.activation(adjT[q][:, b, mt, :], ps_adjT[b][:, mt * N:(mt + 1) * N], ACT.Copy,
                                       accum_out=powers0[:, 1, t:t + 1]).then_inc(adjT_copied, 1)

            def relu_h0(n):
                act.wait_ge(xn0_ready, n + 1)
                act.activation(h0[:], xn0[:], ACT.Relu).then_inc(h0_ready, 1)

            def copy_u(n):
                act.wait_ge(u_done, n + 1)
                act.activation(uT_hi[:], ps_u[:], ACT.Copy).then_inc(uT_hi_ready, 1)

            def relu_h(n, q):
                act.wait_ge(hT_done, n + 1)
                act.activation(hT[q][:], ps_hT[:], ACT.Relu).then_inc(hT_ready, 1)

            copy_adj(0, 0)
            relu_h0(0)
            copy_u(0)
            relu_h(0, 0)
            copy_adj(1, 1)
            relu_h0(1)
            act.wait_ge(wse_in_place, 96)
            act.wait_ge(vectors_ready, 4)
            act.wait_ge(consts_ready, 7)

            def step(i, q):
                act.wait_ge(c1_done, i + 1)
                act.activation(c1[:], ps_c1[:], ACT.Relu, bias=bn_shift[:, 0:1]).then_inc(c1_ready, 1)
                act.wait_ge(s_done, i + 1)
                act.activation(kL[0:32, :], ps_s[0:32, :], ACT.Identity, bias=bse[0:32, :]).then_inc(k_by_act, 1)
                act.activation(kL[32:64, :], ps_s[32:64, :], ACT.Square, bias=bse[32:64, :]).then_inc(k_by_act, 1)
                act.activation(kR[64:96, :], ps_s[64:96, :], ACT.Square, bias=bse[64:96, :]).then_inc(k_by_act, 1)
                if exists(i + 1):
                    copy_u(i + 1)
                for b in range(2):
                    act.wait_ge(kernel_done, 2 * i + b + 1)
                    act.activation(kern[:, b], ps_kernel[b][:].rearrange("p (m n) -> p m n", m=NT),
                                   ACT.Exp).then_inc(kern_ready, 1)
                if exists(i + 1):
                    relu_h(i + 1, 1 - q)
                act.wait_ge(cr_ready, i + 1)
                act.activation(xc_hi[:], cr[:], ACT.Relu).then_inc(xc_hi_ready, 1)
                if exists(i + 2):
                    copy_adj(i + 2, q)
                act.wait_ge(nmp_done, i + 1)
                act.activation(nmp_hi[:], ps_nmp[:], ACT.Copy).then_inc(nmp_hi_ready, 1)
                act.wait_ge(ghn_done, i + 1)
                act.activation(half_ghn[:], ps_ghn[:], ACT.Identity, bias=gate_bias[:, 2:3],
                               scale=0.5).then_inc(half_ghn_ready, 1)
                if exists(i + 2):
                    relu_h0(i + 2)
                act.wait_ge(r_done, i + 1)
                act.activation(tanh_r[:], ps_r[:], ACT.Tanh, bias=gate_bias[:, 0:1],
                               scale=0.5).then_inc(tanh_r_ready, 1)
                act.wait_ge(z_done, i + 1)
                act.activation(tanh_z[:], ps_z[:], ACT.Tanh, bias=gate_bias[:, 1:2],
                               scale=0.5).then_inc(tanh_z_ready, 1)
                act.wait_ge(n_in_ready, i + 1)
                act.activation(n_gate[:], n_in[:], ACT.Tanh, bias=cols[:, IH_N:IH_N + 1]).then_inc(n_ready, 1)

            sweep(act, step)

        @block.vector
        def _(dve):
            def norm_stats(n, source, stats, parts, mean, power, stats_sem):
                for t in range(TILES):
                    dve.bn_stats(stats[:, t, :], source[:, t, :]).then_inc(stats_sem, 1)
                even, odd = stats[:, :, 0:3], stats[:, :, 3:6]
                dve.wait_ge(stats_sem, 10 * n + 4)
                dve.tensor_tensor(parts[:, :, 0:2], even[:, :, 1:3], odd[:, :, 1:3], ALU.add).then_inc(stats_sem, 1)
                dve.tensor_tensor(parts[:, :, 2], even[:, :, 1], odd[:, :, 1], ALU.subtract).then_inc(stats_sem, 1)
                dve.wait_ge(stats_sem, 10 * n + 6)
                dve.tensor_scalar(mean[:], parts[:, :, 0], 0.5, None, ALU.mult).then_inc(stats_sem, 1)
                dve.scalar_tensor_tensor(out=parts[:, :, 3], in0=parts[:, :, 2], scalar=0.25, in1=parts[:, :, 2],
                                         op0=ALU.mult, op1=ALU.mult).then_inc(stats_sem, 1)
                dve.tensor_scalar(parts[:, :, 4], parts[:, :, 1], 1.0 / P, LN_EPS,
                                  ALU.mult, ALU.add).then_inc(stats_sem, 1)
                dve.wait_ge(stats_sem, 10 * n + 9)
                dve.tensor_tensor(power, parts[:, :, 3], parts[:, :, 4], ALU.add).then_inc(stats_sem, 1)

            def stats_x(n, q):
                dve.wait_ge(x_loaded[q], loads_of(n, q))
                norm_stats(n, X[q], stats0, parts0, mean0, powers0[:, 0, :], stats0_ready)

            def norm_x(n, q):
                dve.wait_ge(scale0_ready, n + 1)
                for t in range(TILES):
                    last = dve.tensor_scalar(xn0[:, t, :], X[q][:, t, :], mean0[:, t:t + 1], scale0[:, t:t + 1],
                                             ALU.subtract, ALU.mult)
                last.then_inc(xn0_ready, 1)

            def split_u(n):
                dve.wait_ge(uT_hi_ready, n + 1)
                dve.tensor_tensor(uT_lo[:], ps_u[:], uT_hi[:].bitcast(F32), ALU.subtract).then_inc(uT_lo_ready, 1)

            def residual0(n, q):
                dve.wait_ge(out_done, n + 1)
                dve.wait_ge(xb_ready, n + 1)
                dve.wait_ge(deg_ready, n + 1)
                for t in range(TILES):
                    last = dve.scalar_tensor_tensor(out=X1[q][:, t, :], in0=ps_out[:, t * P:(t + 1) * P],
                                                    scalar=deg[q][:, t:t + 1], in1=xb[:, t, :],
                                                    op0=ALU.mult, op1=ALU.add)
                last.then_inc(x1_ready, 1)
                dve.wait_ge(x1_ready, n + 1)
                norm_stats(n, X1[q], stats1, parts1, mean1, power1[:], stats1_ready)

            def norm_x1(n, q):
                dve.wait_ge(rstd1_ready, n + 1)
                for t in range(TILES):
                    last = dve.tensor_scalar(xn1[:, t, :], X1[q][:, t, :], mean1[:, t:t + 1], rstd1[:, t:t + 1],
                                             ALU.subtract, ALU.mult)
                last.then_inc(xn1_ready, 1)

            def split_h(n, q):
                dve.wait_ge(hT_ready, n + 1)
                dve.tensor_copy(hT_hi[q][:], hT[q][:]).then_inc(hT_hi_ready, 1)

            dve.memset(minus_half[:], -0.5).then_inc(dve_prep, 1)
            dve.memset(ones[:], 1.0).then_inc(consts_ready, 1)
            dve.memset(w_f[:, WS:WS + KQ], 0.0).then_inc(wse_zero, 1)
            dve.memset(bse[:], 0.0).then_inc(wse_zero, 1)
            dve.memset(kL[64:96, :], -1.0).then_inc(consts_ready, 1)
            dve.memset(kR[32:64, :], -1.0).then_inc(consts_ready, 1)
            for part in (c1_hi, c1_lo):
                dve.memset(part[:, :, 0:PAD].bitcast(F32), 0.0).then_inc(consts_ready, 1)
                dve.memset(part[:, :, PAD + N:].bitcast(F32), 0.0).then_inc(consts_ready, 1)
            stats_x(0, 0)
            norm_x(0, 0)
            dve.wait_ge(weights_in[0], 48)
            dve.tensor_copy(w_hi[:, W0:W1], w_f[:, W0:W1]).then_inc(weights_hi, 1)
            dve.wait_ge(weights_hi, 1)
            dve.tensor_tensor(w_lo[:, W0:W1], w_f[:, W0:W1], w_hi[:, W0:W1].bitcast(F32),
                              ALU.subtract).then_inc(weights_lo, 1)
            split_u(0)
            residual0(0, 0)
            dve.wait_ge(x_loaded[1], loads_of(1, 1))
            norm_x1(0, 0)
            split_h(0, 0)
            stats_x(1, 1)
            norm_x(1, 1)
            dve.wait_ge(scaled_cols, 3)
            dve.wait_ge(ident_ready, 1)
            for v in range(2):
                dve.tensor_scalar(bn_diag[:, v, :], ident[:], bn_scale_col[:, v:v + 1], None, ALU.mult).then_inc(diag_ready, 1)
            dve.wait_ge(bn_rows_done, 1)
            dve.tensor_copy(bn_scale_row[:], ps_conv[:, 0:2 * P].rearrange("p (v o) -> p v o", v=2)).then_inc(scaled, 1)
            dve.wait_ge(scaled, 1)
            dve.wait_ge(weights_in[1], 64)
            dve.wait_ge(wse_in_place, 96)
            dve.tensor_tensor(w_f[:, W1:WS], w_f[:, W1:WS], bn_scale_row[:, 0, :], ALU.mult).then_inc(scaled, 1)
            dve.wait_ge(scaled, 2)
            dve.tensor_copy(w_hi[:, W1:W2], w_f[:, W1:W2]).then_inc(weights_hi, 1)
            dve.wait_ge(weights_hi, 2)
            dve.tensor_tensor(w_lo[:, W1:W2], w_f[:, W1:W2], w_hi[:, W1:W2].bitcast(F32),
                              ALU.subtract).then_inc(weights_lo, 1)
            dve.wait_ge(weights_in[2], 16)
            w2_taps = w_f[:, W2:WEND].rearrange("p (k o) -> p k o", k=TAPS)
            dve.tensor_tensor(w2_taps, w2_taps, bn_scale_row[:, 1, :].unsqueeze(1).broadcast_to([P, TAPS, P]),
                              ALU.mult).then_inc(scaled, 1)
            dve.wait_ge(scaled, 3)
            dve.tensor_copy(w_hi[:, W2:WEND], w_f[:, W2:WEND]).then_inc(weights_hi, 1)
            dve.wait_ge(weights_hi, 3)
            dve.tensor_tensor(w_lo[:, W2:WEND], w_f[:, W2:WEND], w_hi[:, W2:WEND].bitcast(F32),
                              ALU.subtract).then_inc(weights_lo, 1)

            def mix(n, q):
                dve.wait_ge(hn_ready, n + 1)
                dve.wait_ge(tanh_z_ready, n + 1)
                dve.scalar_tensor_tensor(out=z_part[:], in0=tanh_z[:], scalar=1.0, in1=h_minus_n[:],
                                         op0=ALU.add, op1=ALU.mult).then_inc(z_part_ready, 1)
                dve.wait_ge(z_part_ready, n + 1)
                dve.scalar_tensor_tensor(out=yT[:], in0=z_part[:], scalar=0.5, in1=n_gate[:],
                                         op0=ALU.mult, op1=ALU.add).then_inc(yT_ready, 1)

            def finish(n, q):
                dve.wait_ge(yT_done, n + 1)
                dve.wait_ge(y_stored[q], loads_of(n, q))
                dve.tensor_tensor(OUT[q][:], ps_yT[:].rearrange("p (t d) -> p t d", t=TILES), X1[q][:],
                                  ALU.add).then_inc(out_ready, 1)

            def step(i, q):
                dve.wait_ge(c1_ready, i + 1)
                dve.tensor_copy(c1_hi[:, :, PAD:PAD + N], c1[:].rearrange("p (b n) -> p b n", b=2)).then_inc(c1_hi_ready, 1)
                dve.wait_ge(k_by_act, 3 * i + 1)
                dve.tensor_scalar(kR[0:32, :], ps_s[0:32, :], bse[0:32, :], 2.0, ALU.add, ALU.mult).then_inc(k_by_dve, 1)
                dve.wait_ge(msg_done, i + 1)
                dve.tensor_tensor(msg_b[:], ps_msg[:].rearrange("p (t d) -> p t d", t=TILES),
                                  rows[:, ROW_BMSG, :].unsqueeze(1).broadcast_to([P, TILES, P]),
                                  ALU.add).then_inc(msg_b_ready, 1)
                if exists(i - 1):
                    mix(i - 1, 1 - q)
                    finish(i - 1, 1 - q)
                if exists(i + 1):
                    split_u(i + 1)
                    residual0(i + 1, 1 - q)
                    norm_x1(i + 1, 1 - q)
                for b in range(2):
                    dve.wait_ge(kern_ready, 2 * i + b + 1)
                    dve.tensor_tensor(edges[:, b], kern[:, b], adjT[q][:, b], ALU.mult).then_inc(edges_ready, 1)
                if exists(i + 2):
                    stats_x(i + 2, q)
                if exists(i + 1):
                    split_h(i + 1, 1 - q)
                dve.wait_ge(conv_done, i + 1)
                dve.scalar_tensor_tensor(out=cr[:], in0=ps_conv[:], scalar=bn_shift[:, 1:2], in1=hT[q][:],
                                         op0=ALU.add, op1=ALU.add).then_inc(cr_ready, 1)
                dve.wait_ge(xc_hi_ready, i + 1)
                dve.scalar_tensor_tensor(out=xc_lo[:], in0=cr[:], scalar=0.0, in1=xc_hi[:].bitcast(F32),
                                         op0=ALU.max, op1=ALU.subtract).then_inc(xc_lo_ready, 1)
                dve.wait_ge(nmp_hi_ready, i + 1)
                dve.tensor_tensor(nmp_lo[:], ps_nmp[:], nmp_hi[:].bitcast(F32), ALU.subtract).then_inc(nmp_lo_ready, 1)
                if exists(i + 2):
                    norm_x(i + 2, q)
                dve.wait_ge(half_ghn_ready, i + 1)
                dve.wait_ge(tanh_r_ready, i + 1)
                dve.scalar_tensor_tensor(out=rg[:], in0=tanh_r[:], scalar=1.0, in1=half_ghn[:],
                                         op0=ALU.add, op1=ALU.mult).then_inc(rg_ready, 1)
                dve.wait_ge(rg_ready, i + 1)
                dve.wait_ge(gin_done, i + 1)
                dve.tensor_tensor(n_in[:], ps_gin[:], rg[:], ALU.add).then_inc(n_in_ready, 1)

            sweep(dve, step)
            mix(PAIRS - 1, (PAIRS - 1) % 2)
            finish(PAIRS - 1, (PAIRS - 1) % 2)

        @block.gpsimd
        def _(pool):
            def roots_x(n, q):
                pool.wait_ge(stats0_ready, 10 * (n + 1))
                pool.wait_ge(adjT_copied, TILES * (n + 1))
                pool.tensor_tensor(roots0[:], powers0[:], minus_half[:], ALU.pow).then_inc(roots0_ready, 1)
                pool.wait_ge(roots0_ready, n + 1)
                pool.tensor_tensor(scale0[:], roots0[:, 0, :], roots0[:, 1, :], ALU.mult).then_inc(scale0_ready, 1)
                pool.tensor_copy(deg[q][:], roots0[:, 1, :]).then_inc(deg_ready, 1)

            def bias_x(n, q):
                pool.wait_ge(x_loaded[q], loads_of(n, q))
                pool.tensor_tensor(xb[:], X[q][:], rows[:, ROW_BIAS0, :].unsqueeze(1).broadcast_to([P, TILES, P]),
                                   ALU.add).then_inc(xb_ready, 1)

            def root_x1(n):
                pool.wait_ge(stats1_ready, 10 * (n + 1))
                pool.tensor_tensor(rstd1[:], power1[:], minus_half[:, 0, 0:TILES], ALU.pow).then_inc(rstd1_ready, 1)

            def split_h(n, q):
                pool.wait_ge(hT_hi_ready, n + 1)
                pool.tensor_tensor(hT_lo[q][:], hT[q][:], hT_hi[q][:].bitcast(F32), ALU.subtract).then_inc(hT_lo_ready, 1)

            pool.memset(ident[:], 0.0).then_inc(pool_prep, 1)
            pool.wait_ge(pool_prep, 1)
            pool.affine_select(out=ident[:], in_=ident[:], compare_op=ALU.not_equal, fill=1.0, base=0,
                               pattern=[[-1, P]], channel_multiplier=1).then_inc(ident_ready, 1)
            pool.wait_ge(dve_prep, 1)
            roots_x(0, 0)
            pool.wait_ge(weights_in[0], 48)
            bias_x(0, 0)
            pool.tensor_scalar(bn_scale_col[:], cols[:, BN1_V:BN2_V + 1:BN2_V - BN1_V], BN_EPS, None,
                               ALU.add).then_inc(pool_prep, 1)
            root_x1(0)
            pool.wait_ge(pool_prep, 2)
            pool.tensor_tensor(bn_scale_col[:], bn_scale_col[:], minus_half[:, 0, 0:2], ALU.pow).then_inc(scaled_cols, 2)
            pool.wait_ge(scaled_cols, 2)
            pool.tensor_tensor(bn_scale_col[:], bn_scale_col[:], cols[:, BN1_G:BN2_G + 1:BN2_G - BN1_G],
                               ALU.mult).then_inc(scaled_cols, 1)
            split_h(0, 0)
            roots_x(1, 1)
            pool.wait_ge(scaled_cols, 3)
            pool.tensor_tensor(bn_shift[:], bn_scale_col[:], cols[:, BN1_M:BN2_M + 1:BN2_M - BN1_M],
                               ALU.mult).then_inc(scaled_cols, 1)
            pool.wait_ge(scaled_cols, 4)
            pool.tensor_tensor(bn_shift[:], cols[:, BN1_B:BN2_B + 1:BN2_B - BN1_B], bn_shift[:],
                               ALU.subtract).then_inc(vectors_ready, 1)
            pool.tensor_tensor(gate_bias[:, 0:2], cols[:, IH_R:IH_Z + 1], cols[:, HH_R:HH_Z + 1],
                               ALU.add).then_inc(scaled_cols, 1)
            pool.wait_ge(scaled_cols, 5)
            pool.tensor_scalar(gate_bias[:, 0:2], gate_bias[:, 0:2], 0.5, None, ALU.mult).then_inc(vectors_ready, 1)
            pool.tensor_scalar(gate_bias[:, 2:3], cols[:, HH_N:HH_N + 1], 0.5, None, ALU.mult).then_inc(vectors_ready, 2)

            def subtract_n(n, q):
                pool.wait_ge(n_ready, n + 1)
                pool.tensor_tensor(h_minus_n[:], hT[q][:], n_gate[:], ALU.subtract).then_inc(hn_ready, 1)

            def step(i, q):
                if exists(i - 1):
                    subtract_n(i - 1, 1 - q)
                pool.wait_ge(c1_hi_ready, i + 1)
                pool.tensor_tensor(c1_lo[:, :, PAD:PAD + N], c1[:].rearrange("p (b n) -> p b n", b=2),
                                   c1_hi[:, :, PAD:PAD + N].bitcast(F32), ALU.subtract).then_inc(c1_lo_ready, 1)
                pool.wait_ge(msg_b_ready, i + 1)
                if exists(i + 1):
                    bias_x(i + 1, 1 - q)
                pool.tensor_scalar(msg[:], msg_b[:], 0.0, None, ALU.max).then_inc(msg_ready, 1)
                if exists(i + 1):
                    root_x1(i + 1)
                    split_h(i + 1, 1 - q)
                if exists(i + 2):
                    roots_x(i + 2, q)

            sweep(pool, step)
            subtract_n(PAIRS - 1, (PAIRS - 1) % 2)


def kernel(x, adj, L0_gnn_weight, L0_gnn_bias, L1_gnn_w_se, L1_gnn_b_se, L1_gnn_conv1_w, L1_gnn_bn1_g, L1_gnn_bn1_b,
           L1_gnn_bn1_m, L1_gnn_bn1_v, L1_gnn_conv2_w, L1_gnn_bn2_g, L1_gnn_bn2_b, L1_gnn_bn2_m, L1_gnn_bn2_v,
           L1_gnn_w_msg, L1_gnn_b_msg, L1_gnn_w_ih, L1_gnn_b_ih, L1_gnn_w_hh, L1_gnn_b_hh):
    import numpy as np
    import concourse.bacc as bacc
    from concourse.bass_utils import run_bass_kernel_spmd

    def a(v):
        return np.asarray(v)

    conv2 = np.transpose(a(L1_gnn_conv2_w), (1, 2, 0)).reshape(P, TAPS * P)
    w_ih = np.transpose(a(L1_gnn_w_ih).T.reshape(2, P, 3 * P), (1, 0, 2))
    b_ih = a(L1_gnn_b_ih).reshape(3, P)
    b_hh = a(L1_gnn_b_hh).reshape(3, P)
    cols = np.stack([a(L1_gnn_bn1_g), a(L1_gnn_bn1_b), a(L1_gnn_bn1_m), a(L1_gnn_bn1_v),
                     a(L1_gnn_bn2_g), a(L1_gnn_bn2_b), a(L1_gnn_bn2_m), a(L1_gnn_bn2_v),
                     b_ih[0], b_ih[1], b_ih[2], b_hh[0], b_hh[1], b_hh[2]], axis=1)
    rows = np.stack([a(L0_gnn_bias), a(L1_gnn_b_msg)], axis=0)
    arrays = {
        "in_x": a(x),
        "in_adj": a(adj),
        "in_w0": a(L0_gnn_weight),
        "in_w1": a(L1_gnn_conv1_w)[:, :, 0].T,
        "in_w2": conv2,
        "in_wse": a(L1_gnn_w_se).T,
        "in_bse": a(L1_gnn_b_se).reshape(-1, 1),
        "in_wmsg": a(L1_gnn_w_msg).T,
        "in_wih": w_ih,
        "in_whh": a(L1_gnn_w_hh).T,
        "in_cols": cols,
        "in_rows": rows,
    }
    arrays = {name: np.ascontiguousarray(v) for name, v in arrays.items()}
    nc = bacc.Bacc("TRN2", target_bir_lowering=False, num_devices=1)
    args = [nc.dram_tensor(name, list(v.shape), mybir.dt.from_np(v.dtype), kind="ExternalInput").ap()
            for name, v in arrays.items()]
    out = nc.dram_tensor("out_y", list(arrays["in_x"].shape), F32, kind="ExternalOutput").ap()
    build_program(nc, *args, out)
    result = run_bass_kernel_spmd(nc, [arrays], core_ids=[0])
    return result.results[0]["out_y"]
```

```python
from contextlib import ExitStack

import concourse.bass as bass
from concourse import mybir

P = 128
TAPS = 17
PAD = TAPS // 2
LN_EPS = 1e-5
BN_EPS = 1e-5

F32 = mybir.dt.float32
F32R = mybir.dt.float32r
ACT = mybir.ActivationFunctionType
ALU = mybir.AluOpType

BN1_G, BN1_B, BN1_M, BN1_V, BN2_G, BN2_B, BN2_M, BN2_V, IH_R, IH_Z, IH_N, HH_R, HH_Z, HH_N = range(14)
ROW_BIAS0, ROW_BMSG = range(2)


def build_program(nc, x, adj, w0_in, w1_in, w2_in, wms_in, wih_in, whh_in, cols_in, rows_in, bse_in, y):
    B, N, D = x.shape
    assert D == P and N == 2 * P and B % 2 == 0
    PAIRS = B // 2
    TILES = 2 * N // P
    NT = N // P
    COLS = 2 * N
    FEATS = bse_in.shape[0]
    MS = P + FEATS

    W1 = 0
    WHH = W1 + P
    WIH = WHH + 3 * P
    W2 = WIH + 6 * P
    WEND = W2 + TAPS * P

    K_SQ = 3 * FEATS
    K_ONE = K_SQ + 2
    K_RIGHT = 32

    with ExitStack() as ctx:
        def sb(name, shape, dt=F32):
            return ctx.enter_context(nc.sbuf_tensor(name, shape, dt))

        def sem(name):
            return ctx.enter_context(nc.semaphore(name))

        psum = ctx.enter_context(nc.psum_tensor("psum", [P, 8, COLS], F32))
        bank = [psum[:, b, :] for b in range(8)]
        ps_c1, ps_ms, ps_u, ps_conv, ps_kT, ps_out = bank[4], psum[:, 5:7, :], bank[1], bank[0], bank[1], bank[7]
        ps_kernel, ps_yT, ps_hT, ps_adjT = bank[2:4], bank[7], bank[1], bank[2:4]
        ps_nmp, ps_ghn, ps_r, ps_z, ps_gin = bank[5], bank[7], bank[4], bank[6], bank[0]
        ps_ms_tiles = ps_ms[:, :, 0:2 * MS].rearrange("p b (t c) -> p b t c", t=2)

        w_f = sb("w_f", [P, WEND])
        w_hi = sb("w_hi", [P, WEND], F32R)
        w_lo = sb("w_lo", [P, WEND], F32R)
        w0 = sb("w0", [P, P])
        wms = sb("wms", [P, MS])
        cols = sb("cols", [P, 14])
        rows = sb("rows", [P, 2, P])
        bse = sb("bse", [P, FEATS])
        bn_scale = sb("bn_scale", [P, 2])
        bn_shift = sb("bn_shift", [P, 2])
        gate_bias = sb("gate_bias", [P, 3])
        minus_half = sb("minus_half", [P, 2, TILES])
        ident = sb("ident", [P, P])

        X = [sb(f"X{q}", [P, TILES, P]) for q in range(2)]
        ADJ = [sb(f"ADJ{q}", [P, 2, NT, N]) for q in range(2)]
        adjT = [sb(f"adjT{q}", [P, 2, NT, N]) for q in range(2)]
        stats0 = sb("stats0", [P, TILES, 6])
        parts0 = sb("parts0", [P, TILES, 5])
        mean0 = sb("mean0", [P, TILES])
        powers0 = sb("powers0", [P, 2, TILES])
        roots0 = sb("roots0", [P, 2, TILES])
        scale0 = sb("scale0", [P, TILES])
        deg = [sb(f"deg{q}", [P, TILES]) for q in range(2)]
        xn0 = sb("xn0", [P, TILES, P])
        h0_hi = sb("h0_hi", [P, TILES, P], F32R)
        h0_lo = sb("h0_lo", [P, TILES, P], F32R)
        adjT_hi = sb("adjT_hi", [P, 2, NT, N], F32R)
        adjT_lo = sb("adjT_lo", [P, 2, NT, N], F32R)
        uT = sb("uT", [P, COLS])
        xb = sb("xb", [P, TILES, P])
        X1 = [sb(f"X1_{q}", [P, TILES, P]) for q in range(2)]

        stats1 = sb("stats1", [P, TILES, 6])
        parts1 = sb("parts1", [P, TILES, 5])
        mean1 = sb("mean1", [P, TILES])
        power1 = sb("power1", [P, TILES])
        rstd1 = sb("rstd1", [P, TILES])
        xn1 = sb("xn1", [P, TILES, P])
        hT = [sb(f"hT{q}", [P, COLS]) for q in range(2)]
        hT_hi = [sb(f"hT_hi{q}", [P, COLS], F32R) for q in range(2)]
        hT_lo = [sb(f"hT_lo{q}", [P, COLS], F32R) for q in range(2)]
        c1 = sb("c1", [P, COLS])
        c1_hi = sb("c1_hi", [P, 2, N + 2 * PAD], F32R)
        c1_lo = sb("c1_lo", [P, 2, N + 2 * PAD], F32R)
        feats = sb("feats", [P, TILES, FEATS])
        feats_sq = sb("feats_sq", [P, TILES, FEATS])
        norm_sq = sb("norm_sq", [P, TILES])
        k_node = sb("k_node", [P, TILES, P], F32R)
        kL = sb("kL", [P, COLS], F32R)
        kR = sb("kR", [P, COLS], F32R)
        msg_b = sb("msg_b", [P, TILES, P])
        msg_hi = sb("msg_hi", [P, TILES, P], F32R)
        msg_lo = sb("msg_lo", [P, TILES, P], F32R)
        kern = sb("kern", [P, 2, NT, N])
        edges = sb("edges", [P, 2, NT, N])
        edges_hi = sb("edges_hi", [P, 2, NT, N], F32R)
        edges_lo = sb("edges_lo", [P, 2, NT, N], F32R)
        h_shift = sb("h_shift", [P, COLS])
        cr = sb("cr", [P, COLS])
        xc_hi = sb("xc_hi", [P, COLS], F32R)
        xc_lo = sb("xc_lo", [P, COLS], F32R)
        nmp_hi = sb("nmp_hi", [P, COLS], F32R)
        nmp_lo = sb("nmp_lo", [P, COLS], F32R)
        half_ghn = sb("half_ghn", [P, COLS])
        tanh_r = sb("tanh_r", [P, COLS])
        tanh_z = sb("tanh_z", [P, COLS])
        rg = sb("rg", [P, COLS])
        n_in = sb("n_in", [P, COLS])
        n_gate = sb("n_gate", [P, COLS])
        h_minus_n = sb("h_minus_n", [P, COLS])
        z_part = sb("z_part", [P, COLS])
        yT = sb("yT", [P, COLS])
        OUT = [sb(f"OUT{q}", [P, TILES, P]) for q in range(2)]

        weights_in = [sem(f"weights_in{c}") for c in range(3)]
        pool_prep, dve_prep, ident_ready, consts_ready = sem("pool_prep"), sem("dve_prep"), sem("ident_ready"), sem("consts_ready")
        weights_hi, weights_lo, vectors_ready = sem("weights_hi"), sem("weights_lo"), sem("vectors_ready")
        x_loaded = [sem(f"x_loaded{q}") for q in range(2)]
        adj_loaded = [sem(f"adj_loaded{q}") for q in range(2)]
        y_stored = [sem(f"y_stored{q}") for q in range(2)]
        adjT_done, u_done, out_done, hT_done = sem("adjT_done"), sem("u_done"), sem("out_done"), sem("hT_done")
        c1_done, msg_done, conv_done, kT_done = sem("c1_done"), sem("msg_done"), sem("conv_done"), sem("kT_done")
        kernel_done, nmp_done, ghn_done = sem("kernel_done"), sem("nmp_done"), sem("ghn_done")
        r_done, z_done, gin_done, yT_done = sem("r_done"), sem("z_done"), sem("gin_done"), sem("yT_done")
        adjT_copied, adjT_hi_ready, h0_hi_ready, uT_ready = sem("adjT_copied"), sem("adjT_hi_ready"), sem("h0_hi_ready"), sem("uT_ready")
        hT_hi_ready, hT_ready, c1_hi_ready, c1_ready = sem("hT_hi_ready"), sem("hT_ready"), sem("c1_hi_ready"), sem("c1_ready")
        kL_ready, kern_ready, msg_hi_ready, edges_hi_ready = sem("kL_ready"), sem("kern_ready"), sem("msg_hi_ready"), sem("edges_hi_ready")
        xc_hi_ready, nmp_hi_ready, half_ghn_ready = sem("xc_hi_ready"), sem("nmp_hi_ready"), sem("half_ghn_ready")
        tanh_r_ready, tanh_z_ready, n_ready = sem("tanh_r_ready"), sem("tanh_z_ready"), sem("n_ready")
        stats0_ready, xn0_ready = sem("stats0_ready"), sem("xn0_ready")
        h0_lo_ready, x1_ready = sem("h0_lo_ready"), sem("x1_ready")
        stats1_ready, xn1_ready = sem("stats1_ready"), sem("xn1_ready")
        k_node_ready, kR_ready, msg_b_ready, msg_lo_ready = sem("k_node_ready"), sem("kR_ready"), sem("msg_b_ready"), sem("msg_lo_ready")
        edges_ready = sem("edges_ready")
        cr_ready, xc_lo_ready, nmp_lo_ready = sem("cr_ready"), sem("xc_lo_ready"), sem("nmp_lo_ready")
        rg_ready, n_in_ready, z_part_ready, yT_ready, out_ready = sem("rg_ready"), sem("n_in_ready"), sem("z_part_ready"), sem("yT_ready"), sem("out_ready")
        deg_ready, roots0_ready, scale0_ready, xb_ready = sem("deg_ready"), sem("roots0_ready"), sem("scale0_ready"), sem("xb_ready")
        rstd1_ready, hT_lo_ready, c1_lo_ready = sem("rstd1_ready"), sem("hT_lo_ready"), sem("c1_lo_ready")
        adjT_lo_ready, edges_lo_ready = sem("adjT_lo_ready"), sem("edges_lo_ready")
        h_shift_ready, hn_ready = sem("h_shift_ready"), sem("hn_ready")

        def loads_of(n, q):
            return 8 * (n - q) + 16

        x_pairs = x.rearrange("(n b) (t p) d -> n p (b t) d", b=2, p=P)
        y_pairs = y.rearrange("(n b) (t p) d -> n p (b t) d", b=2, p=P)
        adj_pairs = adj.rearrange("(n b) (t p) m -> n p b t m", b=2, p=P)

        def sweep(eng, step):
            step(0, 0)
            steady = (PAIRS - 3) // 2 * 2
            with eng.Fori(1, 1 + steady, 2) as i:
                step(i, 1)
                step(i + 1, 0)
            for n in range(1 + steady, PAIRS):
                step(n, n % 2)

        def exists(n):
            return not isinstance(n, int) or 0 <= n < PAIRS

        block = ctx.enter_context(nc.Block())

        @block.sync
        def _(sp):
            def load(n, q):
                sp.dma_start(ADJ[q][:, 0], adj_pairs[n, :, 0]).then_inc(adj_loaded[q], 16)
                sp.dma_start(ADJ[q][:, 1], adj_pairs[n, :, 1]).then_inc(adj_loaded[q], 16)
                sp.dma_start(X[q][:], x_pairs[n]).then_inc(x_loaded[q], 16)

            for q in range(2):
                sp.sem_inc(y_stored[q], 16)
            load(0, 0)
            sp.dma_start(rows[:], rows_in.unsqueeze(0).broadcast_to([P, 2, P])).then_inc(weights_in[0], 16)
            sp.dma_start(w0[:], w0_in).then_inc(weights_in[0], 16)
            sp.dma_start(cols[:], cols_in).then_inc(weights_in[0], 16)
            sp.dma_start(bse[:], bse_in.unsqueeze(0).broadcast_to([P, FEATS])).then_inc(weights_in[0], 16)
            load(1, 1)

            def step(i, q):
                if exists(i + 2):
                    sp.wait_ge(adjT_done, 2 * (i + 1))
                    sp.wait_ge(xn0_ready, i + 1)
                    sp.wait_ge(xb_ready, i + 1)
                    load(i + 2, q)
                if exists(i - 1):
                    sp.wait_ge(out_ready, i)
                    sp.dma_start(y_pairs[i - 1], OUT[1 - q][:]).then_inc(y_stored[1 - q], 16)

            sweep(sp, step)
            sp.wait_ge(out_ready, PAIRS)
            sp.dma_start(y_pairs[PAIRS - 1], OUT[(PAIRS - 1) % 2][:]).then_inc(y_stored[(PAIRS - 1) % 2], 16)
            for q in range(2):
                sp.wait_ge(y_stored[q], 16 * (PAIRS // 2 + 1))

        @block.tensor
        def _(pe):
            def w(part, at, width=P):
                return part[:, at:at + width]

            def product(out, left, right, first, last):
                (lh, ll), (rh, rl) = left, right
                pe.matmul(out, lh, rh, start=first, stop=False)
                pe.matmul(out, ll, rh, start=False, stop=False)
                return pe.matmul(out, lh, rl, start=False, stop=last)

            def weight(at, width=P):
                return w(w_hi, at, width), w(w_lo, at, width)

            def transpose_adj(n, q):
                pe.wait_ge(adj_loaded[q], 2 * loads_of(n, q))
                for b in range(2):
                    pe_bank = ps_adjT[b].rearrange("p (m n) -> p m n", m=NT)
                    for mt in range(NT):
                        for nt in range(NT):
                            last = pe.transpose(pe_bank[:, mt, nt * P:(nt + 1) * P],
                                                ADJ[q][:, b, nt, mt * P:(mt + 1) * P], ident[:])
                    last.then_inc(adjT_done, 1)

            def aggregate(n):
                pe.wait_ge(h0_hi_ready, n + 1)
                pe.wait_ge(adjT_hi_ready, 2 * (n + 1))
                pe.wait_ge(h0_lo_ready, n + 1)
                pe.wait_ge(adjT_lo_ready, 2 * (n + 1))
                for b in range(2):
                    for mt in range(NT):
                        t = b * NT + mt
                        last = product(ps_u[:, b * N:(b + 1) * N], (h0_hi[:, t, :], h0_lo[:, t, :]),
                                       (adjT_hi[:, b, mt, :], adjT_lo[:, b, mt, :]), mt == 0, mt == NT - 1)
                last.then_inc(u_done, 1)

            def project(n):
                pe.wait_ge(uT_ready, n + 1)
                for t in range(TILES):
                    c = slice(t * P, (t + 1) * P)
                    last = pe.matmul(ps_out[:, c], uT[:, c], w0[:], start=True, stop=True)
                last.then_inc(out_done, 1)

            def transpose_h(n):
                pe.wait_ge(xn1_ready, n + 1)
                for t in range(TILES):
                    last = pe.transpose(ps_hT[:, t * P:(t + 1) * P], xn1[:, t, :], ident[:])
                last.then_inc(hT_done, 1)

            def transpose_y(n):
                pe.wait_ge(yT_ready, n + 1)
                for t in range(TILES):
                    last = pe.transpose(ps_yT[:, t * P:(t + 1) * P], yT[:, t * P:(t + 1) * P], ident[:])
                last.then_inc(yT_done, 1)

            def head(n, q):
                pe.wait_ge(hT_hi_ready, n + 1)
                pe.wait_ge(hT_lo_ready, n + 1)
                if exists(n - 1):
                    pe.wait_ge(tanh_r_ready, n)
                product(ps_c1, weight(W1), (hT_hi[q][:], hT_lo[q][:]), True, True).then_inc(c1_done, 1)
                if exists(n - 1):
                    pe.wait_ge(tanh_z_ready, n)
                pe.wait_ge(hT_ready, n + 1)
                for t in range(TILES):
                    last = pe.matmul(ps_ms_tiles[:, t // 2, t % 2, :], hT[q][:, t * P:(t + 1) * P], wms[:],
                                     start=True, stop=True)
                last.then_inc(msg_done, 1)

            def conv(n, a, b):
                for k in range(a, b):
                    part, tap = divmod(k, TAPS)
                    if k == 0:
                        pe.wait_ge(c1_hi_ready, n + 1)
                        if exists(n - 1):
                            pe.wait_ge(n_in_ready, n)
                    if k == TAPS:
                        pe.wait_ge(c1_lo_ready, n + 1)
                    left = w(w_lo if part == 2 else w_hi, W2 + tap * P)
                    right = (c1_lo if part == 1 else c1_hi)[:, :, tap:tap + N]
                    last = pe.matmul(ps_conv.rearrange("p (b n) -> p b n", b=2), left, right,
                                     start=(k == 0), stop=(k == 3 * TAPS - 1))
                if b == 3 * TAPS:
                    last.then_inc(conv_done, 1)

            def transpose_k(n):
                pe.wait_ge(k_node_ready, 11 * (n + 1))
                for t in range(TILES):
                    last = pe.transpose(ps_kT[:, t * P:(t + 1) * P], k_node[:, t, :].bitcast(F32), ident[:])
                last.then_inc(kT_done, 1)

            def distances(n):
                pe.wait_ge(kL_ready, n + 1)
                pe.wait_ge(kR_ready, n + 1)
                for b in range(2):
                    for mt in range(NT):
                        c = b * N + mt * P
                        last = pe.matmul(ps_kernel[b][:, mt * N:(mt + 1) * N], kL[:, c:c + P], kR[:, b * N:(b + 1) * N],
                                         start=True, stop=True)
                    last.then_inc(kernel_done, 1)

            def messages(n):
                pe.wait_ge(edges_hi_ready, 2 * (n + 1))
                pe.wait_ge(edges_lo_ready, 2 * (n + 1))
                pe.wait_ge(msg_lo_ready, n + 1)
                for b in range(2):
                    for mt in range(NT):
                        t = b * NT + mt
                        last = product(ps_nmp[:, b * N:(b + 1) * N], (msg_hi[:, t, :], msg_lo[:, t, :]),
                                       (edges_hi[:, b, mt, :], edges_lo[:, b, mt, :]), mt == 0, mt == NT - 1)
                last.then_inc(nmp_done, 1)

            def gates(n, q):
                hp, cp, mp = (hT_hi[q][:], hT_lo[q][:]), (xc_hi[:], xc_lo[:]), (nmp_hi[:], nmp_lo[:])
                r, z, g = 0, P, 2 * P
                product(ps_ghn, weight(WHH + g), hp, True, True).then_inc(ghn_done, 1)
                product(ps_r, weight(WHH + r), hp, True, False)
                product(ps_z, weight(WHH + z), hp, True, False)
                pe.wait_ge(xc_hi_ready, n + 1)
                pe.wait_ge(xc_lo_ready, n + 1)
                product(ps_r, weight(WIH + r), cp, False, False)
                pe.wait_ge(nmp_hi_ready, n + 1)
                pe.wait_ge(nmp_lo_ready, n + 1)
                product(ps_r, weight(WIH + 3 * P + r), mp, False, True).then_inc(r_done, 1)
                product(ps_z, weight(WIH + z), cp, False, False)
                product(ps_z, weight(WIH + 3 * P + z), mp, False, True).then_inc(z_done, 1)
                product(ps_gin, weight(WIH + g), cp, True, False)
                product(ps_gin, weight(WIH + 3 * P + g), mp, False, True).then_inc(gin_done, 1)

            pe.wait_ge(ident_ready, 1)
            transpose_adj(0, 0)
            aggregate(0)
            pe.wait_ge(weights_in[0], 64)
            project(0)
            transpose_adj(1, 1)
            transpose_h(0)
            pe.wait_ge(weights_in[1], 64)
            pe.wait_ge(weights_lo, 2)
            pe.wait_ge(consts_ready, 8)

            def step(i, q):
                head(i, q)
                if exists(i + 1):
                    pe.wait_ge(hT_ready, i + 1)
                    aggregate(i + 1)
                conv(i, 0, 7)
                if exists(i + 1):
                    pe.wait_ge(uT_ready, i + 2)
                transpose_k(i)
                conv(i, 7, 10)
                if exists(i - 1):
                    pe.wait_ge(half_ghn_ready, i)
                    transpose_y(i - 1)
                conv(i, 10, 15)
                if exists(i + 1):
                    if exists(i - 1):
                        pe.wait_ge(out_ready, i)
                    project(i + 1)
                distances(i)
                conv(i, 15, 3 * TAPS)
                if exists(i + 1):
                    transpose_h(i + 1)
                pe.wait_ge(kern_ready, 2 * (i + 1))
                if exists(i + 2):
                    transpose_adj(i + 2, q)
                messages(i)
                if exists(i + 1):
                    pe.wait_ge(x1_ready, i + 2)
                else:
                    pe.wait_ge(out_ready, i)
                gates(i, q)

            sweep(pe, step)
            transpose_y(PAIRS - 1)

        @block.scalar
        def _(act):
            act.dma_start(w_f[:, W1:W1 + P], w1_in).then_inc(weights_in[1], 16)
            act.dma_start(w_f[:, WHH:WIH], whh_in).then_inc(weights_in[1], 16)
            act.dma_start(w_f[:, WIH:W2].rearrange("p (c g) -> p c g", c=2), wih_in).then_inc(weights_in[1], 16)
            act.dma_start(wms[:], wms_in).then_inc(weights_in[1], 16)
            act.dma_start(w_f[:, W2:WEND], w2_in).then_inc(weights_in[2], 16)

            def copy_adj(n, q):
                for b in range(2):
                    act.wait_ge(adjT_done, 2 * n + b + 1)
                    if b == 0:
                        act.wait_ge(roots0_ready, n)
                    for mt in range(NT):
                        t = b * NT + mt
                        act.activation(adjT[q][:, b, mt, :], ps_adjT[b][:, mt * N:(mt + 1) * N], ACT.Copy,
                                       accum_out=powers0[:, 1, t:t + 1]).then_inc(adjT_copied, 1)

            def split_adj(n):
                for b in range(2):
                    act.activation(adjT_hi[:, b], ps_adjT[b].rearrange("p (m n) -> p m n", m=NT),
                                   ACT.Copy).then_inc(adjT_hi_ready, 1)

            def relu_h0(n):
                act.wait_ge(xn0_ready, n + 1)
                act.activation(h0_hi[:], xn0[:], ACT.Relu).then_inc(h0_hi_ready, 1)

            def copy_u(n):
                act.wait_ge(u_done, n + 1)
                act.activation(uT[:], ps_u, ACT.Copy).then_inc(uT_ready, 1)

            def relu_h(n, q):
                act.wait_ge(hT_done, n + 1)
                act.activation(hT_hi[q][:], ps_hT, ACT.Relu).then_inc(hT_hi_ready, 1)
                act.activation(hT[q][:], ps_hT, ACT.Relu).then_inc(hT_ready, 1)

            copy_adj(0, 0)
            split_adj(0)
            relu_h0(0)
            act.wait_ge(weights_in[1], 64)
            act.activation(w_hi[:, W1:W2], w_f[:, W1:W2], ACT.Copy).then_inc(weights_hi, 1)
            copy_u(0)
            act.wait_ge(weights_in[2], 16)
            act.activation(w_hi[:, W2:WEND], w_f[:, W2:WEND], ACT.Copy).then_inc(weights_hi, 1)
            copy_adj(1, 1)
            split_adj(1)
            relu_h(0, 0)
            relu_h0(1)
            act.wait_ge(vectors_ready, 4)
            act.wait_ge(consts_ready, 8)

            def step(i, q):
                act.wait_ge(c1_done, i + 1)
                bn1 = dict(scale=bn_scale[:, 0:1], bias=bn_shift[:, 0:1])
                act.activation(c1_hi[:, :, PAD:PAD + N], ps_c1.rearrange("p (b n) -> p b n", b=2),
                               ACT.Relu, **bn1).then_inc(c1_hi_ready, 1)
                act.activation(c1[:], ps_c1, ACT.Relu, **bn1).then_inc(c1_ready, 1)
                if exists(i + 1):
                    copy_u(i + 1)
                act.wait_ge(msg_b_ready, i + 1)
                act.activation(msg_hi[:], msg_b[:], ACT.Relu).then_inc(msg_hi_ready, 1)
                act.wait_ge(kT_done, i + 1)
                act.activation(kL[0:32, :], ps_kT[0:32, :], ACT.Copy).then_inc(kL_ready, 1)
                for b in range(2):
                    act.wait_ge(kernel_done, 2 * i + b + 1)
                    act.activation(kern[:, b], ps_kernel[b].rearrange("p (m n) -> p m n", m=NT),
                                   ACT.Exp).then_inc(kern_ready, 1)
                for b in range(2):
                    act.wait_ge(edges_ready, 2 * i + b + 1)
                    act.activation(edges_hi[:, b], edges[:, b], ACT.Copy).then_inc(edges_hi_ready, 1)
                if exists(i + 1):
                    relu_h(i + 1, 1 - q)
                act.wait_ge(cr_ready, i + 1)
                act.activation(xc_hi[:], cr[:], ACT.Relu).then_inc(xc_hi_ready, 1)
                if exists(i + 2):
                    copy_adj(i + 2, q)
                act.wait_ge(nmp_done, i + 1)
                act.activation(nmp_hi[:], ps_nmp, ACT.Copy).then_inc(nmp_hi_ready, 1)
                if exists(i + 2):
                    split_adj(i + 2)
                act.wait_ge(ghn_done, i + 1)
                act.activation(half_ghn[:], ps_ghn, ACT.Identity, bias=gate_bias[:, 2:3],
                               scale=0.5).then_inc(half_ghn_ready, 1)
                act.wait_ge(r_done, i + 1)
                act.activation(tanh_r[:], ps_r, ACT.Tanh, bias=gate_bias[:, 0:1],
                               scale=0.5).then_inc(tanh_r_ready, 1)
                if exists(i + 2):
                    relu_h0(i + 2)
                act.wait_ge(z_done, i + 1)
                act.activation(tanh_z[:], ps_z, ACT.Tanh, bias=gate_bias[:, 1:2],
                               scale=0.5).then_inc(tanh_z_ready, 1)
                act.wait_ge(n_in_ready, i + 1)
                act.activation(n_gate[:], n_in[:], ACT.Tanh, bias=cols[:, IH_N:IH_N + 1]).then_inc(n_ready, 1)

            sweep(act, step)

        @block.vector
        def _(dve):
            def norm_stats(n, source, stats, parts, mean, power, stats_sem):
                for t in range(TILES):
                    dve.bn_stats(stats[:, t, :], source[:, t, :]).then_inc(stats_sem, 1)
                even, odd = stats[:, :, 0:3], stats[:, :, 3:6]
                dve.wait_ge(stats_sem, 10 * n + 4)
                dve.tensor_tensor(parts[:, :, 0:2], even[:, :, 1:3], odd[:, :, 1:3], ALU.add).then_inc(stats_sem, 1)
                dve.tensor_tensor(parts[:, :, 2], even[:, :, 1], odd[:, :, 1], ALU.subtract).then_inc(stats_sem, 1)
                dve.wait_ge(stats_sem, 10 * n + 6)
                dve.tensor_scalar(mean[:], parts[:, :, 0], 0.5, None, ALU.mult).then_inc(stats_sem, 1)
                dve.scalar_tensor_tensor(out=parts[:, :, 3], in0=parts[:, :, 2], scalar=0.25, in1=parts[:, :, 2],
                                         op0=ALU.mult, op1=ALU.mult).then_inc(stats_sem, 1)
                dve.tensor_scalar(parts[:, :, 4], parts[:, :, 1], 1.0 / P, LN_EPS,
                                  ALU.mult, ALU.add).then_inc(stats_sem, 1)
                dve.wait_ge(stats_sem, 10 * n + 9)
                dve.tensor_tensor(power, parts[:, :, 3], parts[:, :, 4], ALU.add).then_inc(stats_sem, 1)

            def stats_x(n, q):
                dve.wait_ge(x_loaded[q], loads_of(n, q))
                norm_stats(n, X[q], stats0, parts0, mean0, powers0[:, 0, :], stats0_ready)

            def norm_x(n, q):
                dve.wait_ge(scale0_ready, n + 1)
                for t in range(TILES):
                    last = dve.tensor_scalar(xn0[:, t, :], X[q][:, t, :], mean0[:, t:t + 1], scale0[:, t:t + 1],
                                             ALU.subtract, ALU.mult)
                last.then_inc(xn0_ready, 1)

            def split_h0(n):
                dve.wait_ge(h0_hi_ready, n + 1)
                dve.scalar_tensor_tensor(out=h0_lo[:], in0=xn0[:], scalar=0.0, in1=h0_hi[:].bitcast(F32),
                                         op0=ALU.max, op1=ALU.subtract).then_inc(h0_lo_ready, 1)

            def residual0(n, q):
                dve.wait_ge(out_done, n + 1)
                dve.wait_ge(xb_ready, n + 1)
                dve.wait_ge(deg_ready, n + 1)
                for t in range(TILES):
                    last = dve.scalar_tensor_tensor(out=X1[q][:, t, :], in0=ps_out[:, t * P:(t + 1) * P],
                                                    scalar=deg[q][:, t:t + 1], in1=xb[:, t, :],
                                                    op0=ALU.mult, op1=ALU.add)
                last.then_inc(x1_ready, 1)
                dve.wait_ge(x1_ready, n + 1)
                norm_stats(n, X1[q], stats1, parts1, mean1, power1[:], stats1_ready)

            def norm_x1(n, q):
                dve.wait_ge(rstd1_ready, n + 1)
                for t in range(TILES):
                    last = dve.tensor_scalar(xn1[:, t, :], X1[q][:, t, :], mean1[:, t:t + 1], rstd1[:, t:t + 1],
                                             ALU.subtract, ALU.mult)
                last.then_inc(xn1_ready, 1)

            def distance_operands(n):
                k = 11 * n
                left_hi, left_lo, left_hi2 = (k_node[:, :, a * FEATS:(a + 1) * FEATS] for a in range(3))
                right_hi = k_node[:, :, K_RIGHT:K_RIGHT + 2 * FEATS].rearrange("p t (a f) -> p t a f", a=2)
                right_lo = k_node[:, :, K_RIGHT + 2 * FEATS:K_RIGHT + 3 * FEATS]
                dve.wait_ge(msg_done, n + 1)
                dve.tensor_tensor(feats[:].rearrange("p (b t) f -> p b t f", b=2), ps_ms_tiles[:, :, :, P:MS],
                                  bse[:].unsqueeze(1).unsqueeze(1).broadcast_to([P, 2, 2, FEATS]),
                                  ALU.add).then_inc(k_node_ready, 1)
                dve.wait_ge(k_node_ready, k + 1)
                dve.tensor_copy(left_hi, feats[:]).then_inc(k_node_ready, 1)
                dve.tensor_tensor(feats_sq[:], feats[:], feats[:], ALU.mult).then_inc(k_node_ready, 1)
                dve.wait_ge(k_node_ready, k + 3)
                dve.tensor_tensor(left_lo, feats[:], left_hi.bitcast(F32), ALU.subtract).then_inc(k_node_ready, 1)
                dve.tensor_reduce(norm_sq[:], feats_sq[:], mybir.AxisListType.X, ALU.add).then_inc(k_node_ready, 1)
                dve.tensor_copy(left_hi2, left_hi.bitcast(F32)).then_inc(k_node_ready, 1)
                dve.tensor_scalar(right_hi, left_hi.bitcast(F32).unsqueeze(2).broadcast_to([P, TILES, 2, FEATS]),
                                  2.0, None, ALU.mult).then_inc(k_node_ready, 1)
                dve.wait_ge(k_node_ready, k + 5)
                dve.tensor_scalar(k_node[:, :, K_SQ], norm_sq[:], -1.0, None, ALU.mult).then_inc(k_node_ready, 1)
                dve.tensor_scalar(right_lo, left_lo.bitcast(F32), 2.0, None, ALU.mult).then_inc(k_node_ready, 1)
                dve.wait_ge(k_node_ready, k + 8)
                dve.scalar_tensor_tensor(out=k_node[:, :, K_SQ + 1], in0=norm_sq[:], scalar=-1.0,
                                         in1=k_node[:, :, K_SQ].bitcast(F32),
                                         op0=ALU.mult, op1=ALU.subtract).then_inc(k_node_ready, 1)
                dve.wait_ge(k_node_ready, k + 10)
                dve.tensor_copy(k_node[:, :, K_RIGHT + K_ONE:K_RIGHT + K_ONE + 2],
                                k_node[:, :, K_SQ:K_SQ + 2].bitcast(F32)).then_inc(k_node_ready, 1)

            dve.memset(minus_half[:], -0.5).then_inc(dve_prep, 1)
            dve.memset(k_node[:].bitcast(F32), 0.0).then_inc(dve_prep, 1)
            for part in (kL, kR):
                dve.memset(part[:].bitcast(F32), 0.0).then_inc(consts_ready, 1)
            for part in (c1_hi, c1_lo):
                dve.memset(part[:, :, 0:PAD].bitcast(F32), 0.0).then_inc(consts_ready, 1)
                dve.memset(part[:, :, PAD + N:].bitcast(F32), 0.0).then_inc(consts_ready, 1)
            dve.wait_ge(dve_prep, 2)
            dve.memset(k_node[:, :, K_ONE:K_ONE + 2].bitcast(F32), 1.0).then_inc(consts_ready, 1)
            dve.memset(k_node[:, :, K_RIGHT + K_SQ:K_RIGHT + K_SQ + 2].bitcast(F32), 1.0).then_inc(consts_ready, 1)
            stats_x(0, 0)
            norm_x(0, 0)
            split_h0(0)
            dve.wait_ge(weights_hi, 1)
            dve.tensor_tensor(w_lo[:, W1:W2], w_f[:, W1:W2], w_hi[:, W1:W2].bitcast(F32),
                              ALU.subtract).then_inc(weights_lo, 1)
            residual0(0, 0)
            norm_x1(0, 0)
            stats_x(1, 1)
            norm_x(1, 1)
            split_h0(1)
            dve.wait_ge(weights_hi, 2)
            dve.tensor_tensor(w_lo[:, W2:WEND], w_f[:, W2:WEND], w_hi[:, W2:WEND].bitcast(F32),
                              ALU.subtract).then_inc(weights_lo, 1)
            dve.wait_ge(vectors_ready, 4)

            def mix(n, q):
                dve.wait_ge(hn_ready, n + 1)
                dve.wait_ge(tanh_z_ready, n + 1)
                dve.scalar_tensor_tensor(out=z_part[:], in0=tanh_z[:], scalar=1.0, in1=h_minus_n[:],
                                         op0=ALU.add, op1=ALU.mult).then_inc(z_part_ready, 1)
                dve.wait_ge(z_part_ready, n + 1)
                dve.scalar_tensor_tensor(out=yT[:], in0=z_part[:], scalar=0.5, in1=n_gate[:],
                                         op0=ALU.mult, op1=ALU.add).then_inc(yT_ready, 1)

            def finish(n, q):
                dve.wait_ge(yT_done, n + 1)
                dve.wait_ge(y_stored[q], loads_of(n, q))
                dve.tensor_tensor(OUT[q][:], ps_yT.rearrange("p (t d) -> p t d", t=TILES), X1[q][:],
                                  ALU.add).then_inc(out_ready, 1)

            def step(i, q):
                distance_operands(i)
                dve.tensor_tensor(msg_b[:].rearrange("p (b t) d -> p b t d", b=2), ps_ms_tiles[:, :, :, 0:P],
                                  rows[:, ROW_BMSG, :].unsqueeze(1).unsqueeze(1).broadcast_to([P, 2, 2, P]),
                                  ALU.add).then_inc(msg_b_ready, 1)
                if exists(i - 1):
                    mix(i - 1, 1 - q)
                dve.wait_ge(kT_done, i + 1)
                dve.tensor_copy(kR[0:32, :], ps_kT[K_RIGHT:K_RIGHT + 32, :]).then_inc(kR_ready, 1)
                dve.wait_ge(msg_hi_ready, i + 1)
                dve.scalar_tensor_tensor(out=msg_lo[:], in0=msg_b[:], scalar=0.0, in1=msg_hi[:].bitcast(F32),
                                         op0=ALU.max, op1=ALU.subtract).then_inc(msg_lo_ready, 1)
                if exists(i - 1):
                    finish(i - 1, 1 - q)
                if exists(i + 1):
                    residual0(i + 1, 1 - q)
                for b in range(2):
                    dve.wait_ge(kern_ready, 2 * i + b + 1)
                    dve.tensor_tensor(edges[:, b], kern[:, b], adjT[q][:, b], ALU.mult).then_inc(edges_ready, 1)
                if exists(i + 1):
                    norm_x1(i + 1, 1 - q)
                if exists(i + 2):
                    stats_x(i + 2, q)
                dve.wait_ge(conv_done, i + 1)
                dve.wait_ge(h_shift_ready, i + 1)
                dve.scalar_tensor_tensor(out=cr[:], in0=ps_conv, scalar=bn_scale[:, 1:2], in1=h_shift[:],
                                         op0=ALU.mult, op1=ALU.add).then_inc(cr_ready, 1)
                dve.wait_ge(xc_hi_ready, i + 1)
                dve.scalar_tensor_tensor(out=xc_lo[:], in0=cr[:], scalar=0.0, in1=xc_hi[:].bitcast(F32),
                                         op0=ALU.max, op1=ALU.subtract).then_inc(xc_lo_ready, 1)
                dve.wait_ge(nmp_hi_ready, i + 1)
                dve.tensor_tensor(nmp_lo[:], ps_nmp, nmp_hi[:].bitcast(F32), ALU.subtract).then_inc(nmp_lo_ready, 1)
                if exists(i + 2):
                    norm_x(i + 2, q)
                dve.wait_ge(half_ghn_ready, i + 1)
                dve.wait_ge(tanh_r_ready, i + 1)
                dve.scalar_tensor_tensor(out=rg[:], in0=tanh_r[:], scalar=1.0, in1=half_ghn[:],
                                         op0=ALU.add, op1=ALU.mult).then_inc(rg_ready, 1)
                if exists(i + 2):
                    split_h0(i + 2)
                dve.wait_ge(rg_ready, i + 1)
                dve.wait_ge(gin_done, i + 1)
                dve.tensor_tensor(n_in[:], ps_gin, rg[:], ALU.add).then_inc(n_in_ready, 1)

            sweep(dve, step)
            mix(PAIRS - 1, (PAIRS - 1) % 2)
            finish(PAIRS - 1, (PAIRS - 1) % 2)

        @block.gpsimd
        def _(pool):
            def roots_x(n, q):
                pool.wait_ge(stats0_ready, 10 * (n + 1))
                pool.wait_ge(adjT_copied, TILES * (n + 1))
                pool.tensor_tensor(roots0[:], powers0[:], minus_half[:], ALU.pow).then_inc(roots0_ready, 1)
                pool.wait_ge(roots0_ready, n + 1)
                pool.tensor_tensor(scale0[:], roots0[:, 0, :], roots0[:, 1, :], ALU.mult).then_inc(scale0_ready, 1)
                pool.tensor_copy(deg[q][:], roots0[:, 1, :]).then_inc(deg_ready, 1)

            def bias_x(n, q):
                pool.wait_ge(x_loaded[q], loads_of(n, q))
                pool.tensor_tensor(xb[:], X[q][:], rows[:, ROW_BIAS0, :].unsqueeze(1).broadcast_to([P, TILES, P]),
                                   ALU.add).then_inc(xb_ready, 1)

            def root_x1(n):
                pool.wait_ge(stats1_ready, 10 * (n + 1))
                pool.tensor_tensor(rstd1[:], power1[:], minus_half[:, 0, 0:TILES], ALU.pow).then_inc(rstd1_ready, 1)

            def split_h(n, q):
                pool.wait_ge(hT_ready, n + 1)
                pool.tensor_tensor(hT_lo[q][:], hT[q][:], hT_hi[q][:].bitcast(F32), ALU.subtract).then_inc(hT_lo_ready, 1)

            def split_adj(n, q):
                for b in range(2):
                    pool.wait_ge(adjT_hi_ready, 2 * n + b + 1)
                    pool.tensor_tensor(adjT_lo[:, b], adjT[q][:, b], adjT_hi[:, b].bitcast(F32),
                                       ALU.subtract).then_inc(adjT_lo_ready, 1)

            pool.memset(ident[:], 0.0).then_inc(pool_prep, 1)
            pool.wait_ge(pool_prep, 1)
            pool.affine_select(out=ident[:], in_=ident[:], compare_op=ALU.not_equal, fill=1.0, base=0,
                               pattern=[[-1, P]], channel_multiplier=1).then_inc(ident_ready, 1)
            pool.wait_ge(dve_prep, 1)
            roots_x(0, 0)
            split_adj(0, 0)
            pool.wait_ge(weights_in[0], 64)
            bias_x(0, 0)
            pool.tensor_scalar(bn_scale[:], cols[:, BN1_V:BN2_V + 1:BN2_V - BN1_V], BN_EPS, None,
                               ALU.add).then_inc(pool_prep, 1)
            root_x1(0)
            roots_x(1, 1)
            split_h(0, 0)
            split_adj(1, 1)
            pool.wait_ge(pool_prep, 2)
            pool.tensor_tensor(bn_scale[:], bn_scale[:], minus_half[:, 0, 0:2], ALU.pow).then_inc(pool_prep, 1)
            pool.wait_ge(pool_prep, 3)
            pool.tensor_tensor(bn_scale[:], bn_scale[:], cols[:, BN1_G:BN2_G + 1:BN2_G - BN1_G],
                               ALU.mult).then_inc(pool_prep, 1)
            pool.wait_ge(pool_prep, 4)
            pool.tensor_tensor(bn_shift[:], bn_scale[:], cols[:, BN1_M:BN2_M + 1:BN2_M - BN1_M],
                               ALU.mult).then_inc(pool_prep, 1)
            pool.wait_ge(pool_prep, 5)
            pool.tensor_tensor(bn_shift[:], cols[:, BN1_B:BN2_B + 1:BN2_B - BN1_B], bn_shift[:],
                               ALU.subtract).then_inc(vectors_ready, 1)
            pool.tensor_tensor(gate_bias[:, 0:2], cols[:, IH_R:IH_Z + 1], cols[:, HH_R:HH_Z + 1],
                               ALU.add).then_inc(pool_prep, 1)
            pool.wait_ge(pool_prep, 6)
            pool.tensor_scalar(gate_bias[:, 0:2], gate_bias[:, 0:2], 0.5, None, ALU.mult).then_inc(vectors_ready, 1)
            pool.tensor_scalar(gate_bias[:, 2:3], cols[:, HH_N:HH_N + 1], 0.5, None, ALU.mult).then_inc(vectors_ready, 2)
            pool.wait_ge(vectors_ready, 4)

            def subtract_n(n, q):
                pool.wait_ge(n_ready, n + 1)
                pool.tensor_tensor(h_minus_n[:], hT[q][:], n_gate[:], ALU.subtract).then_inc(hn_ready, 1)

            def step(i, q):
                if exists(i - 1):
                    subtract_n(i - 1, 1 - q)
                pool.wait_ge(c1_ready, i + 1)
                pool.tensor_tensor(c1_lo[:, :, PAD:PAD + N], c1[:].rearrange("p (b n) -> p b n", b=2),
                                   c1_hi[:, :, PAD:PAD + N].bitcast(F32), ALU.subtract).then_inc(c1_lo_ready, 1)
                if exists(i + 1):
                    bias_x(i + 1, 1 - q)
                pool.tensor_tensor(h_shift[:], hT[q][:], bn_shift[:, 1:2].broadcast_to([P, COLS]),
                                   ALU.add).then_inc(h_shift_ready, 1)
                if exists(i + 1):
                    root_x1(i + 1)
                for b in range(2):
                    pool.wait_ge(edges_hi_ready, 2 * i + b + 1)
                    pool.tensor_tensor(edges_lo[:, b], edges[:, b], edges_hi[:, b].bitcast(F32),
                                       ALU.subtract).then_inc(edges_lo_ready, 1)
                if exists(i + 1):
                    split_h(i + 1, 1 - q)
                if exists(i + 2):
                    roots_x(i + 2, q)
                    split_adj(i + 2, q)

            sweep(pool, step)
            subtract_n(PAIRS - 1, (PAIRS - 1) % 2)


def kernel(x, adj, L0_gnn_weight, L0_gnn_bias, L1_gnn_w_se, L1_gnn_b_se, L1_gnn_conv1_w, L1_gnn_bn1_g, L1_gnn_bn1_b,
           L1_gnn_bn1_m, L1_gnn_bn1_v, L1_gnn_conv2_w, L1_gnn_bn2_g, L1_gnn_bn2_b, L1_gnn_bn2_m, L1_gnn_bn2_v,
           L1_gnn_w_msg, L1_gnn_b_msg, L1_gnn_w_ih, L1_gnn_b_ih, L1_gnn_w_hh, L1_gnn_b_hh):
    import numpy as np
    import concourse.bacc as bacc
    from concourse.bass_utils import run_bass_kernel_spmd

    def a(v):
        return np.asarray(v)

    conv2 = np.transpose(a(L1_gnn_conv2_w), (1, 2, 0)).reshape(P, TAPS * P)
    w_ih = np.transpose(a(L1_gnn_w_ih).T.reshape(2, P, 3 * P), (1, 0, 2))
    b_ih = a(L1_gnn_b_ih).reshape(3, P)
    b_hh = a(L1_gnn_b_hh).reshape(3, P)
    cols = np.stack([a(L1_gnn_bn1_g), a(L1_gnn_bn1_b), a(L1_gnn_bn1_m), a(L1_gnn_bn1_v),
                     a(L1_gnn_bn2_g), a(L1_gnn_bn2_b), a(L1_gnn_bn2_m), a(L1_gnn_bn2_v),
                     b_ih[0], b_ih[1], b_ih[2], b_hh[0], b_hh[1], b_hh[2]], axis=1)
    rows = np.stack([a(L0_gnn_bias), a(L1_gnn_b_msg)], axis=0)
    arrays = {
        "in_x": a(x),
        "in_adj": a(adj),
        "in_w0": a(L0_gnn_weight),
        "in_w1": a(L1_gnn_conv1_w)[:, :, 0].T,
        "in_w2": conv2,
        "in_wms": np.concatenate([a(L1_gnn_w_msg).T, a(L1_gnn_w_se).T], axis=1),
        "in_wih": w_ih,
        "in_whh": a(L1_gnn_w_hh).T,
        "in_cols": cols,
        "in_rows": rows,
        "in_bse": a(L1_gnn_b_se),
    }
    arrays = {name: np.ascontiguousarray(v) for name, v in arrays.items()}
    nc = bacc.Bacc("TRN2", target_bir_lowering=False, num_devices=1)
    args = [nc.dram_tensor(name, list(v.shape), mybir.dt.from_np(v.dtype), kind="ExternalInput").ap()
            for name, v in arrays.items()]
    out = nc.dram_tensor("out_y", list(arrays["in_x"].shape), F32, kind="ExternalOutput").ap()
    build_program(nc, *args, out)
    result = run_bass_kernel_spmd(nc, [arrays], core_ids=[0])
    return result.results[0]["out_y"]
```

```python
from contextlib import ExitStack

import concourse.bass as bass
from concourse import mybir

P = 128
TAPS = 17
PAD = TAPS // 2
HALF = (TAPS + 1) // 2
SHARED = TAPS // 2
CONV = 3 * (2 * HALF + SHARED)
LN_EPS = 1e-5
BN_EPS = 1e-5

F32 = mybir.dt.float32
F32R = mybir.dt.float32r
ACT = mybir.ActivationFunctionType
ALU = mybir.AluOpType

BN1_G, BN1_B, BN1_M, BN1_V, BN2_G, BN2_B, BN2_M, BN2_V, IH_R, IH_Z, IH_N, HH_R, HH_Z, HH_N = range(14)
ROW_BIAS0, ROW_BMSG = range(2)


def build_program(nc, x, adj, w0_in, w1_in, w2_in, wms_in, wih_in, whh_in, cols_in, rows_in, bse_in, y):
    B, N, D = x.shape
    assert D == P and N == 2 * P and B % 2 == 0
    PAIRS = B // 2
    LAST = (PAIRS - 1) % 2
    TILES = 2 * N // P
    NT = N // P
    COLS = 2 * N
    FEATS = bse_in.shape[0]
    MS = P + FEATS

    W1 = 0
    WHH = W1 + P
    WIH = WHH + 3 * P
    W2 = WIH + 6 * P
    DIFFS = W2 + SHARED * P
    WEND = DIFFS + 2 * HALF * P
    PH = N // 2
    PHPAD = PAD // 2
    CSPAD = PHPAD - 1

    K_SQ = 3 * FEATS
    K_ONE = K_SQ + 2
    K_RIGHT = 32

    with ExitStack() as ctx:
        def sb(name, shape, dt=F32):
            return ctx.enter_context(nc.sbuf_tensor(name, shape, dt))

        def sem(name):
            return ctx.enter_context(nc.semaphore(name))

        psum = ctx.enter_context(nc.psum_tensor("psum", [P, 8, COLS], F32))
        bank = [psum[:, b, :] for b in range(8)]
        ps_c1, ps_ms, ps_u, ps_conv, ps_kT, ps_out = bank[4], psum[:, 5:7, :], bank[1], bank[0], bank[1], bank[7]
        ps_kernel, ps_yT, ps_hT, ps_adjT = bank[2:4], bank[7], bank[1], bank[2:4]
        ps_nmp, ps_ghn, ps_r, ps_z, ps_gin = bank[5], bank[7], bank[4], bank[1], bank[0]
        ps_last = (bank[7], bank[5])
        ps_conv_phases = ps_conv.rearrange("p (f c) -> p f c", f=2)
        ps_shared = bank[4][:, 0:N]
        ps_ms_tiles = ps_ms[:, :, 0:2 * MS].rearrange("p b (t c) -> p b t c", t=2)

        w_f = sb("w_f", [P, W2])
        taps = sb("taps", [P, TAPS + 2, P])
        tap_diffs = sb("tap_diffs", [P, 2, HALF, P])
        w_hi = sb("w_hi", [P, WEND], F32R)
        w_lo = sb("w_lo", [P, WEND], F32R)
        w0 = sb("w0", [P, P])
        wms = sb("wms", [P, MS])
        cols = sb("cols", [P, 14])
        rows = sb("rows", [P, 2, P])
        bse = sb("bse", [P, FEATS])
        bn_scale = sb("bn_scale", [P, 2])
        bn_shift = sb("bn_shift", [P, 2])
        gate_bias = sb("gate_bias", [P, 3])
        minus_half = sb("minus_half", [P, TILES])
        ident = sb("ident", [P, P])

        X = [sb(f"X{q}", [P, TILES, P]) for q in range(2)]
        ADJ = [sb(f"ADJ{q}", [P, 2, NT, N]) for q in range(2)]
        adjT = [sb(f"adjT{q}", [P, 2, NT, N]) for q in range(2)]
        stats0 = sb("stats0", [P, TILES, 6])
        parts0 = sb("parts0", [P, TILES, 5])
        mean0 = sb("mean0", [P, TILES])
        powers0 = sb("powers0", [P, 2, TILES])
        roots0 = sb("roots0", [P, 2, TILES])
        scale0 = sb("scale0", [P, TILES])
        deg = [sb(f"deg{q}", [P, TILES]) for q in range(2)]
        xn0 = sb("xn0", [P, TILES, P])
        h0_hi = sb("h0_hi", [P, TILES, P], F32R)
        h0_lo = sb("h0_lo", [P, TILES, P], F32R)
        adjT_hi = sb("adjT_hi", [P, 2, NT, N], F32R)
        adjT_lo = sb("adjT_lo", [P, 2, NT, N], F32R)
        uT = sb("uT", [P, COLS])
        xb = sb("xb", [P, TILES, P])
        X1 = [sb(f"X1_{q}", [P, TILES, P]) for q in range(2)]

        stats1 = sb("stats1", [P, TILES, 6])
        parts1 = sb("parts1", [P, TILES, 5])
        mean1 = sb("mean1", [P, TILES])
        power1 = sb("power1", [P, TILES])
        rstd1 = sb("rstd1", [P, TILES])
        xn1 = sb("xn1", [P, TILES, P])
        hT = [sb(f"hT{q}", [P, COLS]) for q in range(2)]
        hT_hi = [sb(f"hT_hi{q}", [P, COLS], F32R) for q in range(2)]
        hT_lo = [sb(f"hT_lo{q}", [P, COLS], F32R) for q in range(2)]
        c1 = sb("c1", [P, 2, 2, PH + 2])
        c1_hi = sb("c1_hi", [P, 2, 2, PH + 2 * PHPAD], F32R)
        c1_lo = sb("c1_lo", [P, 2, 2, PH + 2 * PHPAD], F32R)
        cs = sb("cs", [P, 2, PH + 1])
        cs_hi = sb("cs_hi", [P, 2, PH + 1 + 2 * CSPAD], F32R)
        cs_lo = sb("cs_lo", [P, 2, PH + 1 + 2 * CSPAD], F32R)
        phase_sums = sb("phase_sums", [P, 2, N])
        feats = sb("feats", [P, TILES, FEATS])
        feats_sq = sb("feats_sq", [P, TILES, FEATS])
        norm_sq = sb("norm_sq", [P, TILES])
        k_node = sb("k_node", [P, TILES, 2 * K_RIGHT], F32R)
        kL = sb("kL", [P, COLS], F32R)
        kR = sb("kR", [P, COLS], F32R)
        msg_b = sb("msg_b", [P, TILES, P])
        msg_hi = sb("msg_hi", [P, TILES, P], F32R)
        msg_lo = sb("msg_lo", [P, TILES, P], F32R)
        kern = sb("kern", [P, 2, NT, N])
        edges = sb("edges", [P, 2, NT, N])
        edges_hi = sb("edges_hi", [P, 2, NT, N], F32R)
        edges_lo = sb("edges_lo", [P, 2, NT, N], F32R)
        h_shift = sb("h_shift", [P, COLS])
        cr = sb("cr", [P, COLS])
        xc_hi = sb("xc_hi", [P, COLS], F32R)
        xc_lo = sb("xc_lo", [P, COLS], F32R)
        nmp_hi = sb("nmp_hi", [P, COLS], F32R)
        nmp_lo = sb("nmp_lo", [P, COLS], F32R)
        half_ghn = sb("half_ghn", [P, COLS])
        tanh_r = sb("tanh_r", [P, COLS])
        tanh_z = sb("tanh_z", [P, COLS])
        rg = sb("rg", [P, COLS])
        n_in = sb("n_in", [P, COLS])
        n_gate = sb("n_gate", [P, COLS])
        h_minus_n = sb("h_minus_n", [P, COLS])
        z_part = sb("z_part", [P, COLS])
        yT = sb("yT", [P, COLS])
        OUT = [sb(f"OUT{q}", [P, TILES, P]) for q in range(2)]

        weights_in = [sem(f"weights_in{c}") for c in range(4)]
        pool_prep, dve_prep, ident_ready, consts_ready = sem("pool_prep"), sem("dve_prep"), sem("ident_ready"), sem("consts_ready")
        taps_padded, odd_diffs_ready, even_diffs_ready = sem("taps_padded"), sem("odd_diffs_ready"), sem("even_diffs_ready")
        weights_hi, weights_lo, pool_weights_lo, vectors_ready = sem("weights_hi"), sem("weights_lo"), sem("pool_weights_lo"), sem("vectors_ready")
        x_loaded = [sem(f"x_loaded{q}") for q in range(2)]
        adj_loaded = [[sem(f"adj_loaded{q}_{b}") for b in range(2)] for q in range(2)]
        y_stored = [sem(f"y_stored{q}") for q in range(2)]
        adjT_done, u_done, out_done, hT_done = sem("adjT_done"), sem("u_done"), sem("out_done"), sem("hT_done")
        phases_done = sem("phases_done")
        c1_done, msg_done, conv_done, kT_done = sem("c1_done"), sem("msg_done"), sem("conv_done"), sem("kT_done")
        kernel_done, nmp_done, ghn_done = sem("kernel_done"), sem("nmp_done"), sem("ghn_done")
        r_done, z_done, gin_done, yT_done = sem("r_done"), sem("z_done"), sem("gin_done"), sem("yT_done")
        adjT_copied, adjT_hi_ready, h0_hi_ready, uT_ready = sem("adjT_copied"), sem("adjT_hi_ready"), sem("h0_hi_ready"), sem("uT_ready")
        hT_hi_ready, hT_ready, c1_hi_ready, c1_ready = sem("hT_hi_ready"), sem("hT_ready"), sem("c1_hi_ready"), sem("c1_ready")
        cs_hi_ready = sem("cs_hi_ready")
        kL_ready, kern_ready, msg_hi_ready, edges_hi_ready = sem("kL_ready"), sem("kern_ready"), sem("msg_hi_ready"), sem("edges_hi_ready")
        xc_hi_ready, nmp_hi_ready, half_ghn_ready = sem("xc_hi_ready"), sem("nmp_hi_ready"), sem("half_ghn_ready")
        tanh_r_ready, tanh_z_ready, n_ready = sem("tanh_r_ready"), sem("tanh_z_ready"), sem("n_ready")
        stats0_ready, xn0_ready = sem("stats0_ready"), sem("xn0_ready")
        h0_lo_ready, x1_ready = sem("h0_lo_ready"), sem("x1_ready")
        stats1_ready, xn1_ready = sem("stats1_ready"), sem("xn1_ready")
        k_node_ready, kR_ready, msg_b_ready, msg_lo_ready = sem("k_node_ready"), sem("kR_ready"), sem("msg_b_ready"), sem("msg_lo_ready")
        edges_ready, phase_sums_ready = sem("edges_ready"), sem("phase_sums_ready")
        cr_ready, xc_lo_ready, nmp_lo_ready = sem("cr_ready"), sem("xc_lo_ready"), sem("nmp_lo_ready")
        rg_ready, n_in_ready, z_part_ready, yT_ready, out_ready = sem("rg_ready"), sem("n_in_ready"), sem("z_part_ready"), sem("yT_ready"), sem("out_ready")
        deg_ready, roots0_ready, scale0_ready, xb_ready = sem("deg_ready"), sem("roots0_ready"), sem("scale0_ready"), sem("xb_ready")
        rstd1_ready, hT_lo_ready, c1_lo_ready = sem("rstd1_ready"), sem("hT_lo_ready"), sem("c1_lo_ready")
        cs_ready, cs_lo_ready = sem("cs_ready"), sem("cs_lo_ready")
        adjT_lo_ready, edges_a_lo_ready, edges_b_lo_ready = sem("adjT_lo_ready"), sem("edges_a_lo_ready"), sem("edges_b_lo_ready")
        h_shift_ready, hn_ready = sem("h_shift_ready"), sem("hn_ready")

        def loads_of(n, q):
            return 8 * (n - q) + 16

        x_pairs = x.rearrange("(n b) (t p) d -> n p (b t) d", b=2, p=P)
        y_pairs = y.rearrange("(n b) (t p) d -> n p (b t) d", b=2, p=P)
        adj_pairs = adj.rearrange("(n b) (t p) m -> n p b t m", b=2, p=P)

        def sweep(eng, step):
            step(0, 0)
            steady = (PAIRS - 3) // 2 * 2
            with eng.Fori(1, 1 + steady, 2) as i:
                step(i, 1)
                step(i + 1, 0)
            for n in range(1 + steady, PAIRS):
                step(n, n % 2)

        def exists(n):
            return not isinstance(n, int) or 0 <= n < PAIRS

        even_taps, shared_taps = taps[:, 1:TAPS + 1:2, :], taps[:, 2:TAPS + 1:2, :]
        shared_taps_hi, shared_taps_lo = (part[:, W2:DIFFS].rearrange("p (k o) -> p k o", k=SHARED)
                                          for part in (w_hi, w_lo))
        diffs_hi, diffs_lo = (part[:, DIFFS:WEND].rearrange("p (f k o) -> p f k o", f=2, k=HALF)
                              for part in (w_hi, w_lo))

        block = ctx.enter_context(nc.Block())

        @block.sync
        def _(sp):
            def load(n, q):
                for b in range(2):
                    sp.dma_start(ADJ[q][:, b], adj_pairs[n, :, b]).then_inc(adj_loaded[q][b], 16)
                sp.dma_start(X[q][:], x_pairs[n]).then_inc(x_loaded[q], 16)

            for q in range(2):
                sp.sem_inc(y_stored[q], 16)
            for b in range(2):
                sp.dma_start(ADJ[0][:, b], adj_pairs[0, :, b]).then_inc(adj_loaded[0][b], 16)
            sp.dma_start(rows[:], rows_in.unsqueeze(0).broadcast_to([P, 2, P])).then_inc(weights_in[0], 16)
            sp.dma_start(w0[:], w0_in).then_inc(weights_in[0], 16)
            load(1, 1)
            sp.dma_start(cols[:], cols_in).then_inc(weights_in[3], 16)
            sp.dma_start(bse[:], bse_in.unsqueeze(0).broadcast_to([P, FEATS])).then_inc(weights_in[3], 16)
            sp.dma_start(w_f[:, W1:W1 + P], w1_in).then_inc(weights_in[1], 16)
            sp.dma_start(w_f[:, WHH:WIH], whh_in).then_inc(weights_in[1], 16)
            sp.dma_start(w_f[:, WIH:W2].rearrange("p (c g) -> p c g", c=2), wih_in).then_inc(weights_in[1], 16)
            sp.dma_start(wms[:], wms_in).then_inc(weights_in[1], 16)
            sp.dma_start(taps[:, 1:TAPS + 1, :].rearrange("p k o -> p (k o)"), w2_in).then_inc(weights_in[2], 16)

            def step(i, q):
                if exists(i + 2):
                    sp.wait_ge(adjT_done, 2 * (i + 1))
                    sp.wait_ge(xn0_ready, i + 1)
                    sp.wait_ge(xb_ready, i + 1)
                    load(i + 2, q)
                if exists(i - 1):
                    sp.wait_ge(out_ready, i)
                    sp.dma_start(y_pairs[i - 1], OUT[1 - q][:]).then_inc(y_stored[1 - q], 16)

            sweep(sp, step)
            for b in range(2):
                t = slice(b * NT, (b + 1) * NT)
                sp.wait_ge(out_ready, PAIRS + b)
                sp.dma_start(y_pairs[PAIRS - 1][:, t, :], OUT[LAST][:, t, :]).then_inc(y_stored[LAST], 16)
            for q in range(2):
                sp.wait_ge(y_stored[q], 16 * (PAIRS // 2 + 1 + (q == LAST)))

        @block.tensor
        def _(pe):
            def w(part, at, width=P):
                return part[:, at:at + width]

            def product(out, left, right, first, last):
                (lh, ll), (rh, rl) = left, right
                pe.matmul(out, lh, rh, start=first, stop=False)
                pe.matmul(out, ll, rh, start=False, stop=False)
                return pe.matmul(out, lh, rl, start=False, stop=last)

            def weight(at, width=P):
                return w(w_hi, at, width), w(w_lo, at, width)

            def transpose_adj(n, q):
                for b in range(2):
                    pe.wait_ge(adj_loaded[q][b], loads_of(n, q))
                    pe_bank = ps_adjT[b].rearrange("p (m n) -> p m n", m=NT)
                    for mt in range(NT):
                        for nt in range(NT):
                            last = pe.transpose(pe_bank[:, mt, nt * P:(nt + 1) * P],
                                                ADJ[q][:, b, nt, mt * P:(mt + 1) * P], ident[:])
                    last.then_inc(adjT_done, 1)

            def aggregate(n):
                pe.wait_ge(h0_hi_ready, n + 1)
                pe.wait_ge(adjT_hi_ready, 2 * (n + 1))
                passes = ((h0_hi, adjT_hi), (h0_hi, adjT_lo), (h0_lo, adjT_hi))
                for b in range(2):
                    for k, (left, right) in enumerate(passes):
                        if b == 0 and k == 1:
                            pe.wait_ge(adjT_lo_ready, 2 * (n + 1))
                        if b == 0 and k == 2:
                            pe.wait_ge(h0_lo_ready, n + 1)
                        for mt in range(NT):
                            last = pe.matmul(ps_u[:, b * N:(b + 1) * N], left[:, b * NT + mt, :], right[:, b, mt, :],
                                             start=(k == 0 and mt == 0), stop=(k == 2 and mt == NT - 1))
                last.then_inc(u_done, 1)

            def project(n):
                pe.wait_ge(uT_ready, n + 1)
                for t in range(TILES):
                    c = slice(t * P, (t + 1) * P)
                    last = pe.matmul(ps_out[:, c], uT[:, c], w0[:], start=True, stop=True)
                last.then_inc(out_done, 1)

            def transpose_h(n):
                pe.wait_ge(xn1_ready, n + 1)
                for t in range(TILES):
                    last = pe.transpose(ps_hT[:, t * P:(t + 1) * P], xn1[:, t, :], ident[:])
                last.then_inc(hT_done, 1)

            def transpose_y(n):
                pe.wait_ge(yT_ready, n + 1)
                for t in range(TILES):
                    last = pe.transpose(ps_yT[:, t * P:(t + 1) * P], yT[:, t * P:(t + 1) * P], ident[:])
                last.then_inc(yT_done, 1)

            def first_conv(n, q):
                pe.wait_ge(hT_hi_ready, n + 1)
                pe.wait_ge(hT_lo_ready, n + 1)
                if exists(n - 1):
                    pe.wait_ge(tanh_r_ready, n)
                product(ps_c1, weight(W1), (hT_hi[q][:], hT_lo[q][:]), True, True).then_inc(c1_done, 1)

            def message_inputs(n, q):
                pe.wait_ge(hT_ready, n + 1)
                for t in range(TILES):
                    last = pe.matmul(ps_ms_tiles[:, t // 2, t % 2, :], hT[q][:, t * P:(t + 1) * P], wms[:],
                                     start=True, stop=True)
                last.then_inc(msg_done, 1)

            def conv(n, a, b):
                for k in range(a, b):
                    own = k < 6 * HALF
                    run, tap = divmod(k, HALF) if own else divmod(k - 6 * HALF, SHARED)
                    if k == 0:
                        pe.wait_ge(c1_hi_ready, 2 * n + 1)
                        if exists(n - 1):
                            pe.wait_ge(n_in_ready, n)
                        if isinstance(n, int) and n == 0:
                            pe.wait_ge(weights_hi, 3)
                    if k == HALF:
                        pe.wait_ge(c1_hi_ready, 2 * n + 2)
                        if isinstance(n, int) and n == 0:
                            pe.wait_ge(weights_hi, 4)
                    if k == 2 * HALF:
                        pe.wait_ge(c1_lo_ready, n + 1)
                    if k == 4 * HALF and isinstance(n, int) and n == 0:
                        pe.wait_ge(weights_lo, 3)
                        pe.wait_ge(pool_weights_lo, 1)
                    if k == 6 * HALF:
                        pe.wait_ge(cs_hi_ready, n + 1)
                        pe.wait_ge(cs_lo_ready, n + 1)
                    if own:
                        part, odd = run // 2, 1 - run % 2
                        at = DIFFS + ((1 - odd) * HALF + tap) * P
                        right = (c1_lo if part == 1 else c1_hi)[:, odd, :, tap:tap + PH]
                        out = ps_conv_phases[:, odd, :]
                    else:
                        part = run
                        at = W2 + tap * P
                        right = (cs_lo if part == 1 else cs_hi)[:, :, tap:tap + PH]
                        out = ps_shared
                    last = pe.matmul(out.rearrange("p (b n) -> p b n", b=2), w(w_lo if part == 2 else w_hi, at), right,
                                     start=k in (0, 6 * HALF), stop=k in (5 * HALF - 1, 6 * HALF - 1, CONV - 1),
                                     skip_group_check=own)
                    if k == 6 * HALF - 1:
                        last.then_inc(phases_done, 1)
                    if k == CONV - 1:
                        last.then_inc(conv_done, 1)

            def transpose_k(n):
                pe.wait_ge(k_node_ready, 11 * (n + 1))
                for b in range(2):
                    last = pe.transpose(ps_kT[:, b * P:(b + 1) * P], k_node[:, b * NT:(b + 1) * NT, :].bitcast(F32), ident[:])
                last.then_inc(kT_done, 1)

            def distances(n):
                pe.wait_ge(kL_ready, NT * (n + 1))
                pe.wait_ge(kR_ready, NT * (n + 1))
                for b in range(2):
                    for mt in range(NT):
                        c = b * N + mt * P
                        last = pe.matmul(ps_kernel[b][:, mt * N:(mt + 1) * N], kL[:, c:c + P], kR[:, b * N:(b + 1) * N],
                                         start=True, stop=True)
                    last.then_inc(kernel_done, 1)

            def messages(n):
                pe.wait_ge(edges_hi_ready, 2 * (n + 1))
                pe.wait_ge(edges_a_lo_ready, n + 1)
                pe.wait_ge(edges_b_lo_ready, n + 1)
                pe.wait_ge(msg_lo_ready, n + 1)
                for b in range(2):
                    for mt in range(NT):
                        t = b * NT + mt
                        last = product(ps_nmp[:, b * N:(b + 1) * N], (msg_hi[:, t, :], msg_lo[:, t, :]),
                                       (edges_hi[:, b, mt, :], edges_lo[:, b, mt, :]), mt == 0, mt == NT - 1)
                last.then_inc(nmp_done, 1)

            def gates(n, q):
                hp, cp, mp = (hT_hi[q][:], hT_lo[q][:]), (xc_hi[:], xc_lo[:]), (nmp_hi[:], nmp_lo[:])
                r, z, g = 0, P, 2 * P
                product(ps_ghn, weight(WHH + g), hp, True, True).then_inc(ghn_done, 1)
                pe.wait_ge(cr_ready, n + 1)
                product(ps_r, weight(WHH + r), hp, True, False)
                if exists(n + 1):
                    pe.wait_ge(hT_ready, n + 2)
                product(ps_z, weight(WHH + z), hp, True, False)
                pe.wait_ge(xc_hi_ready, n + 1)
                pe.wait_ge(xc_lo_ready, n + 1)
                product(ps_r, weight(WIH + r), cp, False, False)
                pe.wait_ge(nmp_hi_ready, n + 1)
                pe.wait_ge(nmp_lo_ready, n + 1)
                product(ps_r, weight(WIH + 3 * P + r), mp, False, True).then_inc(r_done, 1)
                product(ps_gin, weight(WIH + g), cp, True, False)
                product(ps_gin, weight(WIH + 3 * P + g), mp, False, True).then_inc(gin_done, 1)
                product(ps_z, weight(WIH + z), cp, False, False)
                product(ps_z, weight(WIH + 3 * P + z), mp, False, True).then_inc(z_done, 1)

            def keep_busy(count):
                for _ in range(count):
                    pe.matmul(ps_conv[:, 0:P], ident[:], ident[:], start=True, stop=True)

            pe.wait_ge(ident_ready, 1)
            keep_busy(6)
            transpose_adj(0, 0)
            keep_busy(6)
            pe.wait_ge(adjT_hi_ready, 2)
            transpose_adj(1, 1)
            aggregate(0)
            pe.wait_ge(weights_in[0], 32)
            project(0)
            keep_busy(20)
            transpose_h(0)
            keep_busy(7)
            pe.wait_ge(weights_in[1], 64)
            pe.wait_ge(weights_lo, 1)
            pe.wait_ge(consts_ready, 14)

            def step(i, q):
                if exists(i - 1):
                    first_conv(i, q)
                    message_inputs(i, q)
                else:
                    message_inputs(i, q)
                    first_conv(i, q)
                if exists(i + 1):
                    if exists(i - 1):
                        pe.wait_ge(tanh_z_ready, i)
                    aggregate(i + 1)
                conv(i, 0, 13)
                if exists(i + 1):
                    pe.wait_ge(uT_ready, i + 2)
                transpose_k(i)
                conv(i, 13, 20)
                if exists(i - 1):
                    pe.wait_ge(half_ghn_ready, i)
                    transpose_y(i - 1)
                conv(i, 20, 24)
                distances(i)
                conv(i, 24, 28)
                if exists(i + 1):
                    if exists(i - 1):
                        pe.wait_ge(out_ready, i)
                    project(i + 1)
                conv(i, 28, CONV)
                pe.wait_ge(kern_ready, 2 * (i + 1))
                if exists(i + 2):
                    transpose_adj(i + 2, q)
                if exists(i + 1):
                    transpose_h(i + 1)
                messages(i)
                if exists(i + 1):
                    pe.wait_ge(x1_ready, i + 2)
                else:
                    pe.wait_ge(out_ready, i)
                gates(i, q)

            sweep(pe, step)
            for b in range(2):
                pe.wait_ge(yT_ready, PAIRS + b)
                for t in range(NT):
                    c = b * N + t * P
                    last = pe.transpose(ps_last[b][:, t * P:(t + 1) * P], yT[:, c:c + P], ident[:])
                last.then_inc(yT_done, 1)

        @block.scalar
        def _(act):
            act.dma_start(X[0][:], x_pairs[0]).then_inc(x_loaded[0], 16)

            def copy_adj(n, q):
                for b in range(2):
                    act.wait_ge(adjT_done, 2 * n + b + 1)
                    if b == 0:
                        act.wait_ge(roots0_ready, 2 * n)
                    for mt in range(NT):
                        t = b * NT + mt
                        act.activation(adjT[q][:, b, mt, :], ps_adjT[b][:, mt * N:(mt + 1) * N], ACT.Copy,
                                       accum_out=powers0[:, 1, t:t + 1]).then_inc(adjT_copied, 1)

            def split_adj(n):
                for b in range(2):
                    act.activation(adjT_hi[:, b], ps_adjT[b].rearrange("p (m n) -> p m n", m=NT),
                                   ACT.Copy).then_inc(adjT_hi_ready, 1)

            def relu_h0(n):
                act.wait_ge(xn0_ready, n + 1)
                act.activation(h0_hi[:], xn0[:], ACT.Relu).then_inc(h0_hi_ready, 1)

            def copy_u(n):
                act.wait_ge(u_done, n + 1)
                act.activation(uT[:], ps_u, ACT.Copy).then_inc(uT_ready, 1)

            def relu_h(n, q):
                act.wait_ge(hT_done, n + 1)
                act.activation(hT_hi[q][:], ps_hT, ACT.Relu).then_inc(hT_hi_ready, 1)
                act.activation(hT[q][:], ps_hT, ACT.Relu).then_inc(hT_ready, 1)

            def update_gate(n):
                act.wait_ge(z_done, n + 1)
                act.activation(tanh_z[:], ps_z, ACT.Tanh, bias=gate_bias[:, 1:2],
                               scale=0.5).then_inc(tanh_z_ready, 1)

            def new_state(n):
                act.wait_ge(n_in_ready, n + 1)
                act.activation(n_gate[:], n_in[:], ACT.Tanh, bias=cols[:, IH_N:IH_N + 1]).then_inc(n_ready, 1)

            copy_adj(0, 0)
            split_adj(0)
            relu_h0(0)
            copy_adj(1, 1)
            copy_u(0)
            split_adj(1)
            act.wait_ge(weights_in[1], 64)
            act.activation(w_hi[:, W1:W2], w_f[:, W1:W2], ACT.Copy).then_inc(weights_hi, 1)
            act.wait_ge(weights_in[2], 16)
            act.activation(shared_taps_hi, shared_taps, ACT.Copy).then_inc(weights_hi, 1)
            act.wait_ge(odd_diffs_ready, 1)
            act.activation(diffs_hi[:, 0], tap_diffs[:, 0], ACT.Copy).then_inc(weights_hi, 1)
            relu_h0(1)
            relu_h(0, 0)
            act.wait_ge(even_diffs_ready, 1)
            act.activation(diffs_hi[:, 1], tap_diffs[:, 1], ACT.Copy).then_inc(weights_hi, 1)
            act.wait_ge(vectors_ready, 4)
            act.wait_ge(consts_ready, 14)

            def step(i, q):
                act.wait_ge(c1_done, i + 1)
                bn1 = dict(scale=bn_scale[:, 0:1], bias=bn_shift[:, 0:1])
                by_phase = ps_c1.rearrange("p (b n f) -> p f b n", b=2, f=2)
                for f in (1, 0):
                    act.activation(c1_hi[:, f, :, PHPAD:PHPAD + PH], by_phase[:, f], ACT.Relu,
                                   **bn1).then_inc(c1_hi_ready, 1)
                act.activation(c1[:, :, :, 1:1 + PH], by_phase, ACT.Relu, **bn1).then_inc(c1_ready, 1)
                if exists(i + 1):
                    copy_u(i + 1)
                act.wait_ge(kT_done, i + 1)
                kT = ps_kT[:, 0:2 * P].rearrange("p (b n) -> p b n", b=2)
                for side, (part, part_ready) in enumerate(((kL, kL_ready), (kR, kR_ready))):
                    for mt in range(NT):
                        at = (2 * mt + side) * K_RIGHT
                        act.activation(part[0:K_RIGHT, :].rearrange("p (b t n) -> p t b n", b=2, t=NT)[:, mt],
                                       kT[at:at + K_RIGHT], ACT.Copy).then_inc(part_ready, 1)
                act.wait_ge(cs_ready, i + 1)
                act.activation(cs_hi[:, :, CSPAD:CSPAD + PH + 1], cs[:], ACT.Copy).then_inc(cs_hi_ready, 1)
                act.wait_ge(msg_b_ready, i + 1)
                act.activation(msg_hi[:], msg_b[:], ACT.Relu).then_inc(msg_hi_ready, 1)
                for b in range(2):
                    act.wait_ge(kernel_done, 2 * i + b + 1)
                    act.activation(kern[:, b], ps_kernel[b].rearrange("p (m n) -> p m n", m=NT),
                                   ACT.Exp).then_inc(kern_ready, 1)
                for b in range(2):
                    act.wait_ge(edges_ready, 2 * i + b + 1)
                    act.activation(edges_hi[:, b], edges[:, b], ACT.Copy).then_inc(edges_hi_ready, 1)
                if exists(i + 1):
                    relu_h(i + 1, 1 - q)
                act.wait_ge(cr_ready, i + 1)
                act.activation(xc_hi[:], cr[:], ACT.Relu).then_inc(xc_hi_ready, 1)
                act.wait_ge(nmp_done, i + 1)
                act.activation(nmp_hi[:], ps_nmp, ACT.Copy).then_inc(nmp_hi_ready, 1)
                if exists(i + 2):
                    copy_adj(i + 2, q)
                    split_adj(i + 2)
                act.wait_ge(ghn_done, i + 1)
                act.activation(half_ghn[:], ps_ghn, ACT.Identity, bias=gate_bias[:, 2:3],
                               scale=0.5).then_inc(half_ghn_ready, 1)
                act.wait_ge(r_done, i + 1)
                act.activation(tanh_r[:], ps_r, ACT.Tanh, bias=gate_bias[:, 0:1],
                               scale=0.5).then_inc(tanh_r_ready, 1)
                if exists(i + 2):
                    relu_h0(i + 2)
                if exists(i + 1):
                    update_gate(i)
                    new_state(i)
                else:
                    new_state(i)
                    update_gate(i)

            sweep(act, step)

        @block.vector
        def _(dve):
            def measure(source, stats, stats_sem):
                for t in range(TILES):
                    dve.bn_stats(stats[:, t, :], source[:, t, :]).then_inc(stats_sem, 1)

            def combine(n, stats, parts, mean, power, stats_sem):
                even, odd = stats[:, :, 0:3], stats[:, :, 3:6]
                dve.wait_ge(stats_sem, 10 * n + 4)
                dve.tensor_tensor(parts[:, :, 0:2], even[:, :, 1:3], odd[:, :, 1:3], ALU.add).then_inc(stats_sem, 1)
                dve.tensor_tensor(parts[:, :, 2], even[:, :, 1], odd[:, :, 1], ALU.subtract).then_inc(stats_sem, 1)
                dve.wait_ge(stats_sem, 10 * n + 6)
                dve.tensor_scalar(mean[:], parts[:, :, 0], 0.5, None, ALU.mult).then_inc(stats_sem, 1)
                dve.scalar_tensor_tensor(out=parts[:, :, 3], in0=parts[:, :, 2], scalar=0.25, in1=parts[:, :, 2],
                                         op0=ALU.mult, op1=ALU.mult).then_inc(stats_sem, 1)
                dve.tensor_scalar(parts[:, :, 4], parts[:, :, 1], 1.0 / P, LN_EPS,
                                  ALU.mult, ALU.add).then_inc(stats_sem, 1)
                dve.wait_ge(stats_sem, 10 * n + 9)
                dve.tensor_tensor(power, parts[:, :, 3], parts[:, :, 4], ALU.add).then_inc(stats_sem, 1)

            def measure_x(n, q):
                dve.wait_ge(x_loaded[q], loads_of(n, q))
                measure(X[q], stats0, stats0_ready)

            def combine_x(n):
                combine(n, stats0, parts0, mean0, powers0[:, 0, :], stats0_ready)

            def norm_x(n, q):
                dve.wait_ge(scale0_ready, n + 1)
                for t in range(TILES):
                    last = dve.tensor_scalar(xn0[:, t, :], X[q][:, t, :], mean0[:, t:t + 1], scale0[:, t:t + 1],
                                             ALU.subtract, ALU.mult)
                last.then_inc(xn0_ready, 1)

            def split_h0(n):
                dve.wait_ge(h0_hi_ready, n + 1)
                dve.scalar_tensor_tensor(out=h0_lo[:], in0=xn0[:], scalar=0.0, in1=h0_hi[:].bitcast(F32),
                                         op0=ALU.max, op1=ALU.subtract).then_inc(h0_lo_ready, 1)

            def residual0(n, q):
                dve.wait_ge(out_done, n + 1)
                dve.wait_ge(xb_ready, n + 1)
                dve.wait_ge(deg_ready, n + 1)
                for t in range(TILES):
                    last = dve.scalar_tensor_tensor(out=X1[q][:, t, :], in0=ps_out[:, t * P:(t + 1) * P],
                                                    scalar=deg[q][:, t:t + 1], in1=xb[:, t, :],
                                                    op0=ALU.mult, op1=ALU.add)
                last.then_inc(x1_ready, 1)
                dve.wait_ge(x1_ready, n + 1)
                measure(X1[q], stats1, stats1_ready)
                combine(n, stats1, parts1, mean1, power1[:], stats1_ready)

            def norm_x1(n, q):
                dve.wait_ge(rstd1_ready, n + 1)
                for t in range(TILES):
                    last = dve.tensor_scalar(xn1[:, t, :], X1[q][:, t, :], mean1[:, t:t + 1], rstd1[:, t:t + 1],
                                             ALU.subtract, ALU.mult)
                last.then_inc(xn1_ready, 1)

            def distance_operands(n):
                k = 11 * n
                left_hi, left_lo, left_hi2 = (k_node[:, :, a * FEATS:(a + 1) * FEATS] for a in range(3))
                right_hi = k_node[:, :, K_RIGHT:K_RIGHT + 2 * FEATS].rearrange("p t (a f) -> p t a f", a=2)
                right_lo = k_node[:, :, K_RIGHT + 2 * FEATS:K_RIGHT + 3 * FEATS]
                dve.wait_ge(msg_done, n + 1)
                dve.tensor_tensor(feats[:].rearrange("p (b t) f -> p b t f", b=2), ps_ms_tiles[:, :, :, P:MS],
                                  bse[:].unsqueeze(1).unsqueeze(1).broadcast_to([P, 2, 2, FEATS]),
                                  ALU.add).then_inc(k_node_ready, 1)
                dve.wait_ge(k_node_ready, k + 1)
                dve.tensor_copy(left_hi, feats[:]).then_inc(k_node_ready, 1)
                dve.tensor_tensor(feats_sq[:], feats[:], feats[:], ALU.mult).then_inc(k_node_ready, 1)
                dve.wait_ge(k_node_ready, k + 3)
                dve.tensor_tensor(left_lo, feats[:], left_hi.bitcast(F32), ALU.subtract).then_inc(k_node_ready, 1)
                dve.tensor_reduce(norm_sq[:], feats_sq[:], mybir.AxisListType.X, ALU.add).then_inc(k_node_ready, 1)
                dve.tensor_copy(left_hi2, left_hi.bitcast(F32)).then_inc(k_node_ready, 1)
                dve.tensor_scalar(right_hi, left_hi.bitcast(F32).unsqueeze(2).broadcast_to([P, TILES, 2, FEATS]),
                                  2.0, None, ALU.mult).then_inc(k_node_ready, 1)
                dve.wait_ge(k_node_ready, k + 5)
                dve.tensor_scalar(k_node[:, :, K_SQ], norm_sq[:], -1.0, None, ALU.mult).then_inc(k_node_ready, 1)
                dve.tensor_scalar(right_lo, left_lo.bitcast(F32), 2.0, None, ALU.mult).then_inc(k_node_ready, 1)
                dve.wait_ge(k_node_ready, k + 8)
                dve.scalar_tensor_tensor(out=k_node[:, :, K_SQ + 1], in0=norm_sq[:], scalar=-1.0,
                                         in1=k_node[:, :, K_SQ].bitcast(F32),
                                         op0=ALU.mult, op1=ALU.subtract).then_inc(k_node_ready, 1)
                dve.wait_ge(k_node_ready, k + 10)
                dve.tensor_copy(k_node[:, :, K_RIGHT + K_ONE:K_RIGHT + K_ONE + 2],
                                k_node[:, :, K_SQ:K_SQ + 2].bitcast(F32)).then_inc(k_node_ready, 1)

            def split_adj0(b):
                dve.wait_ge(adjT_hi_ready, b + 1)
                dve.tensor_tensor(adjT_lo[:, b], adjT[0][:, b], adjT_hi[:, b].bitcast(F32),
                                  ALU.subtract).then_inc(adjT_lo_ready, 1)

            dve.memset(minus_half[:], -0.5).then_inc(dve_prep, 1)
            dve.memset(k_node[:].bitcast(F32), 0.0).then_inc(dve_prep, 1)
            for part in (kL, kR):
                dve.memset(part[:].bitcast(F32), 0.0).then_inc(consts_ready, 1)
            for part in (c1_hi, c1_lo):
                for at in (0, PHPAD + PH):
                    dve.memset(part[:, :, :, at:at + PHPAD].bitcast(F32), 0.0).then_inc(consts_ready, 1)
            for at in (0, PH + 1):
                dve.memset(c1[:, :, :, at:at + 1], 0.0).then_inc(consts_ready, 1)
            for part in (cs_hi, cs_lo):
                for at in (0, CSPAD + PH + 1):
                    dve.memset(part[:, :, at:at + CSPAD].bitcast(F32), 0.0).then_inc(consts_ready, 1)
            for tap in (0, TAPS + 1):
                dve.memset(taps[:, tap, :], 0.0).then_inc(taps_padded, 1)
            dve.wait_ge(dve_prep, 2)
            dve.memset(k_node[:, :, K_ONE:K_ONE + 2].bitcast(F32), 1.0).then_inc(consts_ready, 1)
            dve.memset(k_node[:, :, K_RIGHT + K_SQ:K_RIGHT + K_SQ + 2].bitcast(F32), 1.0).then_inc(consts_ready, 1)
            measure_x(0, 0)
            combine_x(0)
            split_adj0(0)
            norm_x(0, 0)
            split_adj0(1)
            split_h0(0)
            measure_x(1, 1)
            combine_x(1)
            dve.wait_ge(taps_padded, 2)
            dve.wait_ge(weights_in[2], 16)
            dve.tensor_tensor(tap_diffs[:, 0], even_taps, taps[:, 2:TAPS + 2:2, :], ALU.subtract).then_inc(odd_diffs_ready, 1)
            residual0(0, 0)
            norm_x(1, 1)
            norm_x1(0, 0)
            dve.wait_ge(weights_hi, 1)
            dve.tensor_tensor(w_lo[:, W1:W2], w_f[:, W1:W2], w_hi[:, W1:W2].bitcast(F32),
                              ALU.subtract).then_inc(weights_lo, 1)
            split_h0(1)
            dve.wait_ge(hT_ready, 1)
            dve.tensor_tensor(hT_lo[0][:], hT[0][:], hT_hi[0][:].bitcast(F32), ALU.subtract).then_inc(hT_lo_ready, 1)
            dve.wait_ge(vectors_ready, 4)

            def split_taps():
                dve.wait_ge(weights_hi, 4)
                dve.tensor_tensor(diffs_lo[:, 1], tap_diffs[:, 1], diffs_hi[:, 1].bitcast(F32),
                                  ALU.subtract).then_inc(weights_lo, 1)
                dve.wait_ge(weights_hi, 2)
                dve.tensor_tensor(shared_taps_lo, shared_taps, shared_taps_hi.bitcast(F32), ALU.subtract).then_inc(weights_lo, 1)

            def mix(n, q):
                dve.wait_ge(hn_ready, n + 1)
                dve.wait_ge(tanh_z_ready, n + 1)
                dve.scalar_tensor_tensor(out=z_part[:], in0=tanh_z[:], scalar=1.0, in1=h_minus_n[:],
                                         op0=ALU.add, op1=ALU.mult).then_inc(z_part_ready, 1)
                dve.wait_ge(z_part_ready, n + 1)
                dve.scalar_tensor_tensor(out=yT[:], in0=z_part[:], scalar=0.5, in1=n_gate[:],
                                         op0=ALU.mult, op1=ALU.add).then_inc(yT_ready, 1)

            def finish(n, q):
                dve.wait_ge(yT_done, n + 1)
                dve.wait_ge(y_stored[q], loads_of(n, q))
                dve.tensor_tensor(OUT[q][:], ps_yT.rearrange("p (t d) -> p t d", t=TILES), X1[q][:],
                                  ALU.add).then_inc(out_ready, 1)

            def mask(n, q, b):
                dve.wait_ge(kern_ready, 2 * n + b + 1)
                dve.tensor_tensor(edges[:, b], kern[:, b], adjT[q][:, b], ALU.mult).then_inc(edges_ready, 1)

            def step(i, q):
                if exists(i + 2):
                    measure_x(i + 2, q)
                distance_operands(i)
                dve.tensor_tensor(msg_b[:].rearrange("p (b t) d -> p b t d", b=2), ps_ms_tiles[:, :, :, 0:P],
                                  rows[:, ROW_BMSG, :].unsqueeze(1).unsqueeze(1).broadcast_to([P, 2, 2, P]),
                                  ALU.add).then_inc(msg_b_ready, 1)
                if exists(i - 1):
                    mix(i - 1, 1 - q)
                else:
                    split_taps()
                if exists(i - 1):
                    finish(i - 1, 1 - q)
                dve.wait_ge(msg_hi_ready, i + 1)
                dve.scalar_tensor_tensor(out=msg_lo[:], in0=msg_b[:], scalar=0.0, in1=msg_hi[:].bitcast(F32),
                                         op0=ALU.max, op1=ALU.subtract).then_inc(msg_lo_ready, 1)
                if exists(i + 2):
                    combine_x(i + 2)
                mask(i, q, 0)
                if exists(i + 1):
                    residual0(i + 1, 1 - q)
                mask(i, q, 1)
                if exists(i + 1):
                    norm_x1(i + 1, 1 - q)
                dve.wait_ge(edges_hi_ready, 2 * i + 2)
                dve.tensor_tensor(edges_lo[:, 1], edges[:, 1], edges_hi[:, 1].bitcast(F32),
                                  ALU.subtract).then_inc(edges_b_lo_ready, 1)
                dve.wait_ge(phases_done, i + 1)
                dve.wait_ge(h_shift_ready, i + 1)
                dve.scalar_tensor_tensor(out=phase_sums[:], in0=ps_conv_phases, scalar=bn_scale[:, 1:2],
                                         in1=h_shift[:].rearrange("p (c f) -> p f c", f=2),
                                         op0=ALU.mult, op1=ALU.add).then_inc(phase_sums_ready, 1)
                dve.wait_ge(conv_done, i + 1)
                dve.wait_ge(phase_sums_ready, i + 1)
                dve.scalar_tensor_tensor(out=cr[:].rearrange("p (c f) -> p f c", f=2),
                                         in0=ps_shared.unsqueeze(1).broadcast_to([P, 2, N]), scalar=bn_scale[:, 1:2],
                                         in1=phase_sums[:], op0=ALU.mult, op1=ALU.add).then_inc(cr_ready, 1)
                dve.wait_ge(xc_hi_ready, i + 1)
                dve.scalar_tensor_tensor(out=xc_lo[:], in0=cr[:], scalar=0.0, in1=xc_hi[:].bitcast(F32),
                                         op0=ALU.max, op1=ALU.subtract).then_inc(xc_lo_ready, 1)
                dve.wait_ge(nmp_hi_ready, i + 1)
                dve.tensor_tensor(nmp_lo[:], ps_nmp, nmp_hi[:].bitcast(F32), ALU.subtract).then_inc(nmp_lo_ready, 1)
                if exists(i + 2):
                    norm_x(i + 2, q)
                dve.wait_ge(half_ghn_ready, i + 1)
                dve.wait_ge(tanh_r_ready, i + 1)
                dve.scalar_tensor_tensor(out=rg[:], in0=tanh_r[:], scalar=1.0, in1=half_ghn[:],
                                         op0=ALU.add, op1=ALU.mult).then_inc(rg_ready, 1)
                dve.wait_ge(rg_ready, i + 1)
                dve.wait_ge(gin_done, i + 1)
                dve.tensor_tensor(n_in[:], ps_gin, rg[:], ALU.add).then_inc(n_in_ready, 1)
                if exists(i + 2):
                    split_h0(i + 2)

            sweep(dve, step)
            dve.wait_ge(n_ready, PAIRS)
            dve.tensor_tensor(h_minus_n[:], hT[LAST][:], n_gate[:], ALU.subtract).then_inc(hn_ready, 1)
            dve.wait_ge(hn_ready, PAIRS)
            dve.wait_ge(tanh_z_ready, PAIRS)
            dve.scalar_tensor_tensor(out=z_part[:], in0=tanh_z[:], scalar=1.0, in1=h_minus_n[:],
                                     op0=ALU.add, op1=ALU.mult).then_inc(z_part_ready, 1)
            dve.wait_ge(z_part_ready, PAIRS)
            for b in range(2):
                c = slice(b * N, (b + 1) * N)
                dve.scalar_tensor_tensor(out=yT[:, c], in0=z_part[:, c], scalar=0.5, in1=n_gate[:, c],
                                         op0=ALU.mult, op1=ALU.add).then_inc(yT_ready, 1)
            dve.wait_ge(y_stored[LAST], loads_of(PAIRS - 1, LAST))
            for b in range(2):
                t = slice(b * NT, (b + 1) * NT)
                dve.wait_ge(yT_done, PAIRS + b)
                dve.tensor_tensor(OUT[LAST][:, t, :], ps_last[b][:, 0:N].rearrange("p (t d) -> p t d", t=NT),
                                  X1[LAST][:, t, :], ALU.add).then_inc(out_ready, 1)

        @block.gpsimd
        def _(pool):
            def root_x(n):
                pool.wait_ge(stats0_ready, 10 * (n + 1))
                pool.tensor_tensor(roots0[:, 0, :], powers0[:, 0, :], minus_half[:], ALU.pow).then_inc(roots0_ready, 1)

            def root_degree(n, q):
                pool.wait_ge(adjT_copied, TILES * (n + 1))
                pool.tensor_tensor(roots0[:, 1, :], powers0[:, 1, :], minus_half[:], ALU.pow).then_inc(roots0_ready, 1)
                pool.wait_ge(roots0_ready, 2 * (n + 1))
                pool.tensor_tensor(scale0[:], roots0[:, 0, :], roots0[:, 1, :], ALU.mult).then_inc(scale0_ready, 1)
                pool.tensor_copy(deg[q][:], roots0[:, 1, :]).then_inc(deg_ready, 1)

            def bias_x(n, q):
                pool.wait_ge(x_loaded[q], loads_of(n, q))
                pool.tensor_tensor(xb[:], X[q][:], rows[:, ROW_BIAS0, :].unsqueeze(1).broadcast_to([P, TILES, P]),
                                   ALU.add).then_inc(xb_ready, 1)

            def root_x1(n):
                pool.wait_ge(stats1_ready, 10 * (n + 1))
                pool.tensor_tensor(rstd1[:], power1[:], minus_half[:], ALU.pow).then_inc(rstd1_ready, 1)

            def split_h(n, q):
                pool.wait_ge(hT_ready, n + 1)
                pool.tensor_tensor(hT_lo[q][:], hT[q][:], hT_hi[q][:].bitcast(F32), ALU.subtract).then_inc(hT_lo_ready, 1)

            def split_adj(n, q):
                for b in range(2):
                    pool.wait_ge(adjT_hi_ready, 2 * n + b + 1)
                    pool.tensor_tensor(adjT_lo[:, b], adjT[q][:, b], adjT_hi[:, b].bitcast(F32),
                                       ALU.subtract).then_inc(adjT_lo_ready, 1)

            pool.memset(ident[:], 0.0).then_inc(pool_prep, 1)
            pool.wait_ge(pool_prep, 1)
            pool.affine_select(out=ident[:], in_=ident[:], compare_op=ALU.not_equal, fill=1.0, base=0,
                               pattern=[[-1, P]], channel_multiplier=1).then_inc(ident_ready, 1)
            pool.wait_ge(dve_prep, 1)
            root_x(0)
            root_degree(0, 0)
            pool.wait_ge(weights_in[0], 32)
            bias_x(0, 0)
            pool.wait_ge(weights_in[3], 32)
            pool.tensor_scalar(bn_scale[:], cols[:, BN1_V:BN2_V + 1:BN2_V - BN1_V], BN_EPS, None,
                               ALU.add).then_inc(pool_prep, 1)
            pool.wait_ge(pool_prep, 2)
            pool.tensor_tensor(bn_scale[:], bn_scale[:], minus_half[:, 0:2], ALU.pow).then_inc(pool_prep, 1)
            pool.wait_ge(pool_prep, 3)
            pool.tensor_tensor(bn_scale[:], bn_scale[:], cols[:, BN1_G:BN2_G + 1:BN2_G - BN1_G],
                               ALU.mult).then_inc(pool_prep, 1)
            pool.wait_ge(pool_prep, 4)
            pool.tensor_tensor(bn_shift[:], bn_scale[:], cols[:, BN1_M:BN2_M + 1:BN2_M - BN1_M],
                               ALU.mult).then_inc(pool_prep, 1)
            pool.wait_ge(pool_prep, 5)
            pool.tensor_tensor(bn_shift[:], cols[:, BN1_B:BN2_B + 1:BN2_B - BN1_B], bn_shift[:],
                               ALU.subtract).then_inc(vectors_ready, 1)
            pool.tensor_tensor(gate_bias[:, 0:2], cols[:, IH_R:IH_Z + 1], cols[:, HH_R:HH_Z + 1],
                               ALU.add).then_inc(pool_prep, 1)
            pool.wait_ge(pool_prep, 6)
            pool.tensor_scalar(gate_bias[:, 0:2], gate_bias[:, 0:2], 0.5, None, ALU.mult).then_inc(vectors_ready, 1)
            pool.tensor_scalar(gate_bias[:, 2:3], cols[:, HH_N:HH_N + 1], 0.5, None, ALU.mult).then_inc(vectors_ready, 2)
            root_x(1)
            root_degree(1, 1)
            split_adj(1, 1)
            root_x1(0)
            pool.wait_ge(taps_padded, 2)
            pool.wait_ge(weights_in[2], 16)
            pool.tensor_tensor(tap_diffs[:, 1], even_taps, taps[:, 0:TAPS:2, :], ALU.subtract).then_inc(even_diffs_ready, 1)
            pool.wait_ge(weights_hi, 3)
            pool.tensor_tensor(diffs_lo[:, 0], tap_diffs[:, 0], diffs_hi[:, 0].bitcast(F32),
                               ALU.subtract).then_inc(pool_weights_lo, 1)
            pool.wait_ge(vectors_ready, 4)

            def subtract_n(n, q):
                pool.wait_ge(n_ready, n + 1)
                pool.tensor_tensor(h_minus_n[:], hT[q][:], n_gate[:], ALU.subtract).then_inc(hn_ready, 1)

            def step(i, q):
                if exists(i - 1):
                    subtract_n(i - 1, 1 - q)
                pool.wait_ge(c1_ready, i + 1)
                pool.tensor_tensor(c1_lo[:, :, :, PHPAD:PHPAD + PH], c1[:, :, :, 1:1 + PH],
                                   c1_hi[:, :, :, PHPAD:PHPAD + PH].bitcast(F32), ALU.subtract).then_inc(c1_lo_ready, 1)
                pool.tensor_tensor(cs[:], c1[:, 0, :, 1:PH + 2], c1[:, 1, :, 0:PH + 1], ALU.add).then_inc(cs_ready, 1)
                if exists(i + 1):
                    bias_x(i + 1, 1 - q)
                pool.wait_ge(cs_hi_ready, i + 1)
                pool.tensor_tensor(cs_lo[:, :, CSPAD:CSPAD + PH + 1], cs[:], cs_hi[:, :, CSPAD:CSPAD + PH + 1].bitcast(F32),
                                   ALU.subtract).then_inc(cs_lo_ready, 1)
                pool.tensor_tensor(h_shift[:], hT[q][:], bn_shift[:, 1:2].broadcast_to([P, COLS]),
                                   ALU.add).then_inc(h_shift_ready, 1)
                if exists(i + 2):
                    root_x(i + 2)
                pool.wait_ge(edges_hi_ready, 2 * i + 1)
                pool.tensor_tensor(edges_lo[:, 0], edges[:, 0], edges_hi[:, 0].bitcast(F32),
                                   ALU.subtract).then_inc(edges_a_lo_ready, 1)
                if exists(i + 1):
                    root_x1(i + 1)
                if exists(i + 1):
                    split_h(i + 1, 1 - q)
                if exists(i + 2):
                    root_degree(i + 2, q)
                    split_adj(i + 2, q)

            sweep(pool, step)


def kernel(x, adj, L0_gnn_weight, L0_gnn_bias, L1_gnn_w_se, L1_gnn_b_se, L1_gnn_conv1_w, L1_gnn_bn1_g, L1_gnn_bn1_b,
           L1_gnn_bn1_m, L1_gnn_bn1_v, L1_gnn_conv2_w, L1_gnn_bn2_g, L1_gnn_bn2_b, L1_gnn_bn2_m, L1_gnn_bn2_v,
           L1_gnn_w_msg, L1_gnn_b_msg, L1_gnn_w_ih, L1_gnn_b_ih, L1_gnn_w_hh, L1_gnn_b_hh):
    import numpy as np
    import concourse.bacc as bacc
    from concourse.bass_utils import run_bass_kernel_spmd

    def a(v):
        return np.asarray(v)

    conv2 = np.transpose(a(L1_gnn_conv2_w), (1, 2, 0)).reshape(P, TAPS * P)
    w_ih = np.transpose(a(L1_gnn_w_ih).T.reshape(2, P, 3 * P), (1, 0, 2))
    b_ih = a(L1_gnn_b_ih).reshape(3, P)
    b_hh = a(L1_gnn_b_hh).reshape(3, P)
    cols = np.stack([a(L1_gnn_bn1_g), a(L1_gnn_bn1_b), a(L1_gnn_bn1_m), a(L1_gnn_bn1_v),
                     a(L1_gnn_bn2_g), a(L1_gnn_bn2_b), a(L1_gnn_bn2_m), a(L1_gnn_bn2_v),
                     b_ih[0], b_ih[1], b_ih[2], b_hh[0], b_hh[1], b_hh[2]], axis=1)
    rows = np.stack([a(L0_gnn_bias), a(L1_gnn_b_msg)], axis=0)
    arrays = {
        "in_x": a(x),
        "in_adj": a(adj),
        "in_w0": a(L0_gnn_weight),
        "in_w1": a(L1_gnn_conv1_w)[:, :, 0].T,
        "in_w2": conv2,
        "in_wms": np.concatenate([a(L1_gnn_w_msg).T, a(L1_gnn_w_se).T], axis=1),
        "in_wih": w_ih,
        "in_whh": a(L1_gnn_w_hh).T,
        "in_cols": cols,
        "in_rows": rows,
        "in_bse": a(L1_gnn_b_se),
    }
    arrays = {name: np.ascontiguousarray(v) for name, v in arrays.items()}
    nc = bacc.Bacc("TRN2", target_bir_lowering=False, num_devices=1)
    args = [nc.dram_tensor(name, list(v.shape), mybir.dt.from_np(v.dtype), kind="ExternalInput").ap()
            for name, v in arrays.items()]
    out = nc.dram_tensor("out_y", list(arrays["in_x"].shape), F32, kind="ExternalOutput").ap()
    build_program(nc, *args, out)
    result = run_bass_kernel_spmd(nc, [arrays], core_ids=[0])
    return result.results[0]["out_y"]
```
